# Optimizing a Trainium2 kernel written in Bass

```python
import numpy as np
import jax
import jax.numpy as jnp

def _softmax(x, axis=-1):
    return jax.nn.softmax(x, axis=axis)

def _gelu(x):
    return jax.nn.gelu(x, approximate=True)

def _silu(x):
    return jax.nn.silu(x)

def _sigmoid(x):
    return jax.nn.sigmoid(x)

def _layernorm(x, axis=-1, eps=1e-05):
    m = jnp.mean(x, axis=axis, keepdims=True)
    v = jnp.var(x, axis=axis, keepdims=True)
    return (x - m) / jnp.sqrt(v + eps)

def _scatter_add(tgt, idx, src, axis=0):
    return tgt.at[idx].add(src)

def _segment_sum(src, seg, n):
    return jax.ops.segment_sum(src, seg, n)
kernel_name = 'mk_adj_preln_d2_adj_r2_16781a'

def setup_inputs(seed: int=0):
    np.random.seed(seed)
    _w = jnp.asarray

    def _rec_inputs():
        import jax
        import jax.numpy as jnp
        _gk = jax.random.key(seed)
        x = -0.0002928 + 1 * jax.random.normal(jax.random.fold_in(_gk, 1), (4096, 256), jnp.float32)
        _a = jax.random.bernoulli(jax.random.fold_in(_gk, 2), 0.000976562, (4096, 4096))
        _af = _a.astype(jnp.float32)
        adj = _af
        return (x, adj)
    x, adj = _rec_inputs()

    def _L0_gnn_setup():
        import jax, jax.numpy as jnp
        import numpy as np
        N = 4096
        D_IN = 256
        D_OUT = 256
        NEG_BIG = -9000000000000000.0
        key = jax.random.key(seed)
        kx, ka, kw, kb, kn, ke = jax.random.split(key, 6)
        x = jax.random.normal(kx, (N, D_IN), dtype=jnp.float32)
        adj = (jax.random.uniform(ka, (N, N)) > 0.9).astype(jnp.float32)
        stdv = 1.0 / np.sqrt(D_OUT)
        weight = jax.random.uniform(kw, (D_IN, D_OUT), minval=-stdv, maxval=stdv, dtype=jnp.float32)
        bias = jax.random.uniform(kb, (D_OUT,), minval=-stdv, maxval=stdv, dtype=jnp.float32)
        node_w = jax.random.uniform(kn, (D_IN, 1), minval=-1.0, maxval=1.0, dtype=jnp.float32)
        stdv_e = 1.0 / np.sqrt(D_IN)
        edge_w = jax.random.uniform(ke, (D_IN, D_IN), minval=-stdv_e, maxval=stdv_e, dtype=jnp.float32)
        return {'x': x, 'adj': adj, 'weight': weight, 'bias': bias, 'node_w': node_w, 'edge_w': edge_w}
    _L0_gnn_all = _L0_gnn_setup()
    _L0_gnn_in = {k: v for k, v in _L0_gnn_all.items() if k in ('weight', 'bias', 'node_w', 'edge_w')}
    del _L0_gnn_all

    def _L1_gnn_setup():
        import jax, jax.numpy as jnp
        import numpy as np
        N = 4096
        DIN = 256
        DOUT = 256
        key = jax.random.key(seed)
        k1, k2, k3 = jax.random.split(key, 3)
        H_in = jax.random.normal(k1, (N, DIN), dtype=jnp.float32)
        u = jax.random.uniform(k2, (N, N), dtype=jnp.float32)
        upper = (u < 0.005).astype(jnp.float32)
        upper = jnp.triu(upper, k=1)
        A = upper + upper.T
        limit = np.sqrt(6.0 / (DIN + DOUT)).astype(np.float32)
        W = jax.random.uniform(k3, (DIN, DOUT), dtype=jnp.float32, minval=-limit, maxval=limit)
        return {'H_in': H_in, 'A': A, 'W': W}
    _L1_gnn_all = _L1_gnn_setup()
    _L1_gnn_in = {k: v for k, v in _L1_gnn_all.items() if k in ('W',)}
    del _L1_gnn_all
    return {'x': x, 'adj': adj, 'L0_gnn_weight': _L0_gnn_in['weight'], 'L0_gnn_bias': _L0_gnn_in['bias'], 'L0_gnn_node_w': _L0_gnn_in['node_w'], 'L0_gnn_edge_w': _L0_gnn_in['edge_w'], 'L1_gnn_W': _L1_gnn_in['W']}

def reference(x, adj, L0_gnn_weight, L0_gnn_bias, L0_gnn_node_w, L0_gnn_edge_w, L1_gnn_W):
    import jax
    import jax.numpy as jnp

    def _L0_gnn_ref(x, adj, weight, bias, node_w, edge_w):
        import jax, jax.numpy as jnp
        import numpy as np
        N = 4096
        D_IN = 256
        D_OUT = 256
        NEG_BIG = -9000000000000000.0
        node_att = jax.nn.softmax(x @ node_w, axis=0)
        h = x @ edge_w
        e = h @ h.T
        e = jnp.where(adj > 0, e, NEG_BIG)
        edge_att = jax.nn.softmax(e, axis=1)
        combined_att = node_att * edge_att
        support = x @ weight
        output = adj * combined_att @ support
        return output + bias

    def _L1_gnn_ref(H_in, A, W):
        import jax, jax.numpy as jnp
        import numpy as np
        N = 4096
        DIN = 256
        DOUT = 256
        A_ = A + jnp.eye(A.shape[0], dtype=A.dtype)
        d_inv_sqrt = jax.lax.rsqrt(A_.sum(axis=1))
        A_norm = A_ * d_inv_sqrt[:, None] * d_inv_sqrt[None, :]
        H_out = jnp.matmul(jnp.matmul(A_norm, H_in), W)
        return jax.nn.relu(H_out)
    h = jnp.maximum(_layernorm(x, axis=-1), 0.0)
    x = x + _L0_gnn_ref(h, adj, L0_gnn_weight, L0_gnn_bias, L0_gnn_node_w, L0_gnn_edge_w)
    h = jnp.maximum(_layernorm(x, axis=-1), 0.0)
    x = x + _L1_gnn_ref(h, adj, L1_gnn_W)
    return x

_drawn_inputs = setup_inputs


def setup_inputs(seed=0):
    import zlib

    import numpy as np

    out = dict(_drawn_inputs(seed))
    spreads = {}
    factors = {'L0_gnn_weight': 8.0, 'L0_gnn_node_w': 8.0, 'L0_gnn_edge_w': 8.0}
    for name, (base, spread) in spreads.items():
        noise = np.random.default_rng([zlib.crc32(name.encode()), seed]).standard_normal(out[name].shape)
        drawn = base * np.exp(spread * noise) if base else spread * noise
        out[name] = jnp.asarray(drawn.astype(out[name].dtype))
    for name, factor in factors.items():
        out[name] = (out[name] * factor).astype(out[name].dtype)
    return out
```

```python
from contextlib import ExitStack

import concourse.bass as bass
from concourse import mybir

F32 = mybir.dt.float32
BF16 = mybir.dt.bfloat16
I32 = mybir.dt.int32
U32 = mybir.dt.uint32
ALU = mybir.AluOpType
ACT = mybir.ActivationFunctionType
AX = mybir.AxisListType

P = 128
N = 4096
D = 256
T = N // P
KC = D // P
SC = 512
NS = N // SC
NEG_BIG = -9000000000000000.0
EPS = 1e-5


RMAX = bass.bass_isa.ReduceOp.max
RADD = bass.bass_isa.ReduceOp.add

NQ = 4
QC = N // NQ
SEG_CAP = 8
L = NQ * SEG_CAP
CH = 5
EDGES = CH * P
NONE = 2 * N
SLOTS = 4
ABUF = 3
GRP = 8
GW = D + 1


class Signal:

    def __init__(self, sem, per=1):
        self.sem, self.per = sem, per

    def by(self, ins):
        return ins.then_inc(self.sem, 1)

    def wait(self, eng, t, k=None):
        eng.wait_ge(self.sem, t * self.per + (self.per if k is None else k))


def edge_path(nc, flag, x, adj, w0, bias, node_w, edge_w, w1, out, table0, table1):
    adj_q = adj.rearrange("(t p) (q c) -> t p q c", p=P, q=NQ)
    x_t = x.rearrange("(t p) d -> p t d", p=P)
    t0_t = table0.rearrange("(t p) d -> p t d", p=P)
    t1_t = table1.rearrange("(t p) d -> p t d", p=P)
    out_t = out.rearrange("(t p) d -> t p d", p=P)
    ctx = ExitStack()
    with ctx:
        def sb(name, shape, dt=F32):
            return ctx.enter_context(nc.sbuf_tensor(name, shape, dt))

        def bank(name):
            return ctx.enter_context(nc.psum_tensor(name, [P, SC], F32))

        def sem(name):
            return ctx.enter_context(nc.semaphore(name))

        def sig(name, per=1):
            return Signal(sem(name), per)

        X = sb("X", [P, T, D])
        G = sb("G", [P, T, GW])
        A = sb("A", [P, ABUF, NQ, QC + SEG_CAP])
        NBR = sb("NBR", [P, T, CH], U32)
        ROW = sb("ROW", [P, T, CH])
        DEG = sb("DEG", [P, T])
        ENDS = sb("ENDS", [P, T])
        SQ = sb("SQ", [P, T, 2])
        NATT = sb("NATT", [P, T])
        MV = sb("MV", [P, T, 2])
        VE = sb("VE", [P, GRP, 2])
        RT2 = sb("RT2", [P, GRP, 2])
        RSTD = sb("RSTD", [P, T])
        NEGM = sb("NEGM", [P, T])
        DINV = sb("DINV", [P, T])
        MZ = sb("MZ", [P, KC, GW])
        EW = sb("EW", [P, KC, D])
        EWT = sb("EWT", [P, KC, D])
        W0 = sb("W0", [P, KC, D])
        W1 = sb("W1", [P, KC, D])
        BIAS = sb("BIAS", [1, D])
        ones_row = sb("ones_row", [1, P])
        ones8 = sb("ones8", [P, SEG_CAP])
        col1 = sb("col1", [P, P])
        par1 = sb("par1", [P, 1])
        ident = sb("ident", [P, P])
        below = sb("below", [P, P])
        epos = sb("epos", [P, EDGES])
        eown = sb("eown", [P, CH, L])
        nbase = sb("nbase", [P, NQ, SEG_CAP])
        IDX = sb("IDX", [P, SLOTS, NQ, SEG_CAP], U32)
        VAL = sb("VAL", [P, SLOTS, L])
        CUM = sb("CUM", [P, SLOTS, L])
        LST = sb("LST", [P, SLOTS, 2 * L + 1])
        HALF = sb("HALF", [P, SLOTS, 1])
        NEGC = sb("NEGC", [P, SLOTS, 1])
        DIST = sb("DIST", [P, EDGES])
        R = sb("R", [P, SLOTS, EDGES])
        RT = sb("RT", [P, SLOTS, CH, P])
        RW = sb("RW", [P, 2, CH, P])
        HJ = sb("HJ", [P, SLOTS, CH, D])
        MAT = sb("MAT", [P, SLOTS, CH, L])
        tl = sb("tl", [P, CH, L])
        js = sb("js", [P, CH])
        prod = sb("prod", [P, D])
        sc = sb("sc", [P, SLOTS, CH])
        SM = sb("SM", [P, SLOTS, CH, L])
        tw = sb("tw", [P, CH, L])
        WE = sb("WE", [P, SLOTS, CH])
        PEN = sb("PEN", [P, SLOTS, L])
        SR = sb("SR", [P, L])
        EX = sb("EX", [P, L])
        WR = sb("WR", [P, SLOTS, L])
        mx = sb("mx", [P, 1])
        nmx = sb("nmx", [P, 1])
        es = sb("es", [P, 1])
        rs = sb("rs", [P, 1])
        rn = sb("rn", [P, 1])
        ZT = sb("ZT", [P, 2, KC, P])
        st = sb("st", [P, 2, 6])
        HST = HJ[:].rearrange("p s c d -> p (s c d)")[:, 0:2 * GRP * D].rearrange("p (b t d) -> p b t d", b=2, t=GRP)
        junk = sb("junk", [P, NQ // 2, QC], BF16)
        Y2 = sb("Y2", [P, 2, D])
        OT = sb("OT", [P, 2, D])
        zs = sb("zs", [P, 8])
        badm = sb("badm", [P, T])
        badn = sb("badn", [P, T])

        bI, bS, bW, bZ, bO, bP = (bank(f"bank{i}") for i in range(6))
        bG = [bank("bank6"), bank("bank7")]

        in_w = sem("weights_in")
        in_x = [sem(f"x_in{i}") for i in range(T // GRP)]
        in_a = [sem(f"adj_in{i}") for i in range(ABUF)]
        c_pool = sem("pool_constants")
        c_dve = sem("dve_constants")
        c_mem = sem("slots_cleared")
        ewt_ps, ewt_sb, m_ps, m_sb = (sem(n) for n in ("edge_w_turned", "edge_w_T_kept", "m_product", "m_kept"))
        stat0, aggr0 = sig("stats0"), sig("means0")
        ve0, sq0, rstd0, negm0 = (sig(n) for n in ("var0", "root0", "rstd0", "negmean0"))
        h0, turned0, ht0, g_ps, g_sb = (sig(n) for n in ("h0", "h0_turned", "h0T_kept", "g_product", "g_kept"))
        stored0 = [sem(f"table0_stored{i}") for i in range(2)]
        z_dve, z_pool, z_act = sem("node_dve"), sem("node_pool"), sem("node_act")
        found, checked = sig("found", NQ), sig("squares_summed", 2)
        valid, node, count, prefix = sig("valid"), sig("node_listed"), sig("counted"), sig("prefix")
        place, half, negc, dist, rmat = sig("placed"), sig("half"), sig("negcentre"), sig("distance"), sig("rows_matrix")
        listed, match, jm, jr, nbr, row = (sig(n) for n in ("listed", "match", "nbr_masked", "nbr_summed", "nbr", "edge_row"))
        gath = [sem(f"gathered{i}") for i in range(SLOTS)]
        rtm = sig("edge_matrix")
        gexp = sig("g_at_edges", 3)
        score, scm = sig("scores", CH), sig("scores_placed")
        srow, smask, smax, snmax = sig("scores_by_row"), sig("scores_masked"), sig("row_max"), sig("row_negmax")
        expd, inv, rn_, wrow = sig("exponentials"), sig("row_inverse"), sig("row_scale"), sig("row_weights")
        wed, wm, wsum, rw = sig("weights_at_edges"), sig("weights_masked"), sig("edge_weight"), sig("weighted_matrix")
        zt_ps, zt_sb, o_ps, x1, stat1, aggr1 = (sig(n) for n in ("z_product", "z_kept", "o_product", "x1", "stats1", "means1"))
        ve1, sq1, inv1, rd1, nm1 = (sig(n) for n in ("var1", "root1", "inverse1", "scale1", "negmean1"))
        h1 = sig("h1")
        stored1 = sem("table1_stored")
        end_d, end_p = sem("flag_dve"), sem("flag_pool")
        g1 = [sem(f"gathered_again{i}") for i in range(SLOTS)]
        rt1, y_ps, y_sb, o1_ps, o1_sb, o_add = (sig(n) for n in ("edge_matrix1", "y_product", "y_kept", "o1_product", "o1_kept", "o1_added"))
        stored = [sem(f"out_stored{i}") for i in range(2)]
        NGRP = T // GRP
        block = ctx.enter_context(nc.Block())

        def keep1(sp, i):
            h1.wait(sp, (i + 1) * GRP - 1)
            sp.dma_start(t1_t[:, i * GRP:(i + 1) * GRP, :], G[:, i * GRP:(i + 1) * GRP, 0:D]).then_inc(stored1, 16)

        def g_keep(a, t):
            g_ps.wait(a, t)
            g_sb.by(nc.scalar.copy(G[:, t, :], (bO, bZ)[t % 2][:, 0:GW]))

        @block.sync
        def _(sp):
            for i in range(NGRP):
                g = slice(i * GRP, (i + 1) * GRP)
                sp.dma_start(X[:, g, :], x_t[:, g, :]).then_inc(in_x[i], 16)
                if i == 0:
                    for dst, src in ((EW, edge_w), (W0, w0), (W1, w1)):
                        sp.dma_start(dst[:], src.rearrange("(c p) n -> p c n", p=P)).then_inc(in_w, 16)
                    with nc.allow_non_contiguous_dma(reason="256 values of the node weights"):
                        sp.dma_start(MZ[:, :, D:GW], node_w.rearrange("(c p) o -> p c o", p=P)).then_inc(in_w, 16)
                    sp.dma_start(BIAS[:], bias.rearrange("(o n) -> o n", o=1)).then_inc(in_w, 16)

            def load(t):
                if t >= ABUF:
                    found.wait(sp, t - ABUF)
                    checked.wait(sp, t - ABUF)
                sp.dma_start(A[:, t % ABUF, :, 0:QC], adj_q[t]).then_inc(in_a[t % ABUF], 16)

            for t in range(ABUF):
                load(t)
            for i in range(NGRP):
                h0.wait(sp, (i + 1) * GRP - 1)
                sp.dma_start(t0_t[:, i * GRP:(i + 1) * GRP, :], HST[:, i % 2]).then_inc(stored0[i % 2], 16)
            for t in range(ABUF, T):
                load(t)
                if t % GRP == GRP - 1 and t >= 3 * GRP - 1:
                    keep1(sp, t // GRP - 2)
            for i in range(NGRP - 2, NGRP):
                keep1(sp, i)
            for t in range(T):
                o_add.wait(sp, t)
                sp.dma_start(out_t[t], OT[:, t % 2, :]).then_inc(stored[t % 2], 16)
            for s in stored:
                sp.wait_ge(s, 16 * (T // 2))

        @block.gpsimd
        def _(g):
            f = dict(allow_small_or_imprecise_dtypes=True)
            g.iota(col1[:], pattern=[[1, P]], base=1, channel_multiplier=0, **f).then_inc(c_pool, 1)
            g.iota(par1[:], pattern=[[0, 1]], base=1, channel_multiplier=1, **f).then_inc(c_pool, 1)
            g.iota(epos[:], pattern=[[1, EDGES]], base=0, channel_multiplier=0, **f).then_inc(c_pool, 1)
            g.iota(eown[:], pattern=[[P, CH], [0, L]], base=1, channel_multiplier=1, **f).then_inc(c_pool, 1)
            g.iota(nbase[:], pattern=[[-QC, NQ], [0, SEG_CAP]], base=NONE, channel_multiplier=0, **f).then_inc(c_pool, 1)
            g.wait_ge(z_dve, 2)
            g.partition_all_reduce(zs[:, 1:2], zs[:, 0:1], P, RMAX).then_inc(z_pool, 1)
            g.wait_ge(z_act, 1)
            g.partition_all_reduce(zs[:, 4:5], zs[:, 3:4], P, RADD).then_inc(z_pool, 1)
            for s in stored0:
                g.wait_ge(s, 16 * (NGRP // 2))
            turned0.wait(g, T - 1)
            g.memset(HJ[:], 0.0).then_inc(c_mem, 1)
            g.wait_ge(c_mem, 1)
            for t in range(T):
                nbr.wait(g, t)
                if t >= SLOTS:
                    zt_ps.wait(g, t - SLOTS)
                for c in range(CH):
                    g.indirect_dma_start(out=HJ[:, t % SLOTS, c, :], out_offset=None, in_=table0,
                                         in_offset=bass.IndirectOffsetOnAxis(ap=NBR[:, t, c:c + 1], axis=0),
                                         bounds_check=N - 1, oob_is_err=False).then_inc(gath[t % SLOTS], 16)
            g.wait_ge(stored1, 16 * NGRP)
            for t in range(T):
                if t < SLOTS:
                    zt_ps.wait(g, T - SLOTS + t)
                else:
                    y_ps.wait(g, t - SLOTS)
                for c in range(CH):
                    g.indirect_dma_start(out=HJ[:, t % SLOTS, c, :], out_offset=None, in_=table1,
                                         in_offset=bass.IndirectOffsetOnAxis(ap=NBR[:, t, c:c + 1], axis=0),
                                         bounds_check=N - 1, oob_is_err=False).then_inc(g1[t % SLOTS], 16)
            g.wait_ge(end_d, 4)
            g.partition_all_reduce(zs[:, 7:8], zs[:, 6:7], P, RMAX).then_inc(end_p, 1)

        @block.vector
        def _(v):
            V = nc.vector
            V.memset(ones8[:], 1.0).then_inc(c_dve, 1)
            V.memset(A[:, :, :, QC:], 1.0).then_inc(c_dve, 1)
            V.memset(ones_row[:], 1.0).then_inc(c_dve, 1)
            v.wait_ge(c_pool, 5)
            V.tensor_scalar(ident[:], col1[:], par1[:], None, ALU.is_equal).then_inc(c_dve, 1)
            V.tensor_scalar(below[:], col1[:], par1[:], None, ALU.is_gt).then_inc(c_dve, 1)
            for s in range(SLOTS):
                V.tensor_copy(LST[:, s, 2 * L:], par1[:]).then_inc(c_dve, 1)
            v.wait_ge(ewt_ps, 1)
            V.tensor_copy(EWT[:].rearrange("p c n -> p (c n)"), bW[:]).then_inc(ewt_sb, 1)
            v.wait_ge(m_ps, 1)
            v.wait_ge(in_w, 80)
            V.tensor_copy(MZ[:, :, 0:D], bI[:].rearrange("p (c n) -> p c n", c=KC)).then_inc(m_sb, 1)

            def stats0(i):
                gs = slice(i * GRP, (i + 1) * GRP)
                v.wait_ge(in_x[i], 16)
                for t in range(i * GRP, (i + 1) * GRP):
                    stat0.by(V.bn_stats(st[:, t % 2, :], X[:, t, :]))
                    stat0.wait(v, t)
                    aggr0.by(V.bn_aggr(MV[:, t, :], st[:, t % 2, :]))
                aggr0.wait(v, (i + 1) * GRP - 1)
                ve0.by(V.tensor_scalar_add(VE[:, :, 0], MV[:, gs, 1], EPS))
                sq0.wait(v, i)
                rstd0.by(V.reciprocal(RSTD[:, gs], RT2[:, :, 0]))
                rstd0.wait(v, i)
                negm0.by(V.scalar_tensor_tensor(NEGM[:, gs], MV[:, gs, 0], -1.0, RSTD[:, gs], ALU.mult, ALU.mult))

            for i in range(NGRP):
                stats0(i)
                for t in range(i * GRP, (i + 1) * GRP):
                    turned0.wait(v, t)
                    if t >= 2:
                        g_ps.wait(v, t - 2)
                    ht0.by(V.tensor_copy(RW[:, t % 2, 0:KC, :].rearrange("p c n -> p (c n)"), (bS, bW)[t % 2][:, 0:D]))
            g_sb.wait(v, T - 1)
            V.reduce_max(zs[:, 0:1], G[:, :, D], AX.X).then_inc(z_dve, 2)
            v.wait_ge(z_pool, 1)
            V.tensor_scalar_mul(zs[:, 2:3], zs[:, 1:2], -1.0).then_inc(z_dve, 1)
            v.wait_ge(z_pool, 2)
            V.reciprocal(zs[:, 5:6], zs[:, 4:5]).then_inc(z_dve, 1)
            v.wait_ge(z_dve, 4)
            V.tensor_scalar_mul(NATT[:], NATT[:], zs[:, 5:6]).then_inc(z_dve, 1)
            v.wait_ge(z_dve, 5)

            def find(t, q):
                if q == 0:
                    v.wait_ge(in_a[t % ABUF], 16 * (t // ABUF + 1))
                    if t >= SLOTS:
                        node.wait(v, t - SLOTS)
                found.by(V.max_index(IDX[:, t % SLOTS, q, :], ones8[:], A[:, t % ABUF, q, :]))

            def number(t):
                s = t % SLOTS
                found.wait(v, t)
                valid.by(V.tensor_scalar(VAL[:, s, :], IDX[:, s].rearrange("p q k -> p (q k)"), float(QC), None, ALU.is_lt))
                node.by(V.tensor_tensor(LST[:, s, L:2 * L].rearrange("p (q k) -> p q k", q=NQ), nbase[:], IDX[:, s], ALU.subtract))
                valid.wait(v, t)
                count.by(V.tensor_tensor_scan(CUM[:, s, :], VAL[:, s, :], VAL[:, s, :], 0.0, ALU.add, ALU.bypass))

            def positions(t):
                s = t % SLOTS
                deg = CUM[:, s, L - 1:L]
                prefix.wait(v, t)
                place.by(V.scalar_tensor_tensor(LST[:, s, 0:L], CUM[:, s, :], bP[:, 0:1], VAL[:, s, :], ALU.add, ALU.mult))
                V.tensor_copy(DEG[:, t:t + 1], deg)
                V.tensor_tensor(ENDS[:, t:t + 1], deg, bP[:, 0:1], ALU.add)
                half.by(V.tensor_scalar(HALF[:, s, :], deg, 0.5, -0.5, ALU.mult, ALU.add))
                half.wait(v, t)
                negc.by(V.tensor_scalar(NEGC[:, s, :], bP[:, 0:1], HALF[:, s, :], -1.0, ALU.add, ALU.mult))

            def rows_matrix(t):
                dist.wait(v, t)
                rmat.by(V.tensor_scalar(R[:, t % SLOTS, :], DIST[:], HALF[:, t % SLOTS, :], None, ALU.is_le))

            def lists(t):
                s = t % SLOTS
                pl = bI[:, 0:CH * (2 * L + 1)].rearrange("p (c k) -> p c k", c=CH)
                listed.wait(v, t)
                match.by(V.tensor_tensor(MAT[:, s], pl[:, :, 0:L], eown[:], ALU.is_equal))
                row.by(V.tensor_copy(ROW[:, t, :], pl[:, :, 2 * L]))
                match.wait(v, t)
                jm.by(V.tensor_tensor(tl[:], pl[:, :, L:2 * L], MAT[:, s], ALU.mult))
                jm.wait(v, t)
                jr.by(V.reduce_sum(js[:], tl[:], AX.X))
                jr.wait(v, t)
                nbr.by(V.tensor_scalar(NBR[:, t, :], js[:], -1.0, float(NONE), ALU.mult, ALU.add))

            def edge_matrix(t, signal):
                for c in range(CH):
                    ins = V.tensor_scalar(RT[:, t % SLOTS, c, :], col1[:], ROW[:, t, c:c + 1], None, ALU.is_equal)
                signal.by(ins)

            def scores(t, c):
                s = t % SLOTS
                n = 3 * t + c // 2
                gexp.wait(v, t, c // 2 + 1)
                v.wait_ge(gath[s], 16 * CH * (t // SLOTS + 1))
                if 5 * t + c >= 1:
                    v.wait_ge(score.sem, 5 * t + c)
                score.by(V.tensor_tensor_reduce(out=prod[:], in0=bG[n % 2][:, (c % 2) * D:(c % 2 + 1) * D],
                                                in1=HJ[:, s, c, :], scale=1.0, scalar=0.0, op0=ALU.mult, op1=ALU.add,
                                                accum_out=sc[:, s, c:c + 1]))

            def place_scores(t):
                s = t % SLOTS
                score.wait(v, t)
                V.tensor_scalar(PEN[:, s, :], VAL[:, s, :], -NEG_BIG, NEG_BIG, ALU.mult, ALU.add)
                scm.by(V.tensor_tensor(SM[:, s], MAT[:, s], sc[:, s, :].unsqueeze(2).broadcast_to([P, CH, L]), ALU.mult))

            def row_max(t):
                s = t % SLOTS
                srow.wait(v, t)
                smask.by(V.tensor_tensor(SR[:], bS[:, 0:L], PEN[:, s, :], ALU.add))
                smask.wait(v, t)
                smax.by(V.reduce_max(mx[:], SR[:], AX.X))
                smax.wait(v, t)
                snmax.by(V.tensor_scalar_mul(nmx[:], mx[:], -1.0))

            def row_weights(t):
                s = t % SLOTS
                expd.wait(v, t)
                inv.by(V.reciprocal(rs[:], es[:]))
                inv.wait(v, t)
                rn_.by(V.tensor_tensor(rn[:], rs[:], NATT[:, t:t + 1], ALU.mult))
                rn_.wait(v, t)
                wrow.by(V.scalar_tensor_tensor(WR[:, s, :], EX[:], rn[:], VAL[:, s, :], ALU.mult, ALU.mult))

            def edge_weights(t):
                s = t % SLOTS
                wed.wait(v, t)
                wm.by(V.tensor_tensor(tw[:], bW[:, 0:CH * L].rearrange("p (c k) -> p c k", c=CH), MAT[:, s], ALU.mult))
                wm.wait(v, t)
                wsum.by(V.reduce_sum(WE[:, s, :], tw[:], AX.X))

            def residual(t):
                o_ps.wait(v, t)
                x1.by(V.tensor_tensor(X[:, t, :], X[:, t, :], bO[:, 0:D], ALU.add))
                x1.wait(v, t)
                stat1.by(V.bn_stats(st[:, t % 2, :], X[:, t, :]))
                stat1.wait(v, t)
                aggr1.by(V.bn_aggr(MV[:, t, :], st[:, t % 2, :]))

            def norm_a(i):
                gs = slice(i * GRP, (i + 1) * GRP)
                aggr1.wait(v, (i + 1) * GRP - 1)
                V.tensor_scalar_add(VE[:, :, 0], MV[:, gs, 1], EPS)
                ve1.by(V.tensor_scalar_add(VE[:, :, 1], DEG[:, gs], 1.0))

            def norm_b(i):
                gs = slice(i * GRP, (i + 1) * GRP)
                sq1.wait(v, i)
                inv1.by(V.reciprocal(RT2[:], RT2[:]))
                inv1.wait(v, i)
                V.tensor_copy(DINV[:, gs], RT2[:, :, 1])
                rd1.by(V.tensor_tensor(RSTD[:, gs], RT2[:, :, 0], RT2[:, :, 1], ALU.mult))
                rd1.wait(v, i)
                nm1.by(V.scalar_tensor_tensor(NEGM[:, gs], MV[:, gs, 0], -1.0, RSTD[:, gs], ALU.mult, ALU.mult))

            for i in range(T + 4):
                a, u, w, y = i < T, 0 <= i - 1 < T, 0 <= i - 3 < T, 0 <= i - 4 < T
                if a:
                    find(i, 0)
                if u:
                    number(i - 1)
                if w:
                    edge_matrix(i - 3, rtm)
                    scores(i - 3, 0)
                    scores(i - 3, 1)
                if u:
                    positions(i - 1)
                if a:
                    find(i, 1)
                if w:
                    for c in range(2, CH):
                        scores(i - 3, c)
                    place_scores(i - 3)
                if u:
                    rows_matrix(i - 1)
                if a:
                    find(i, 2)
                if w:
                    row_max(i - 3)
                if u:
                    lists(i - 1)
                if w:
                    row_weights(i - 3)
                if a:
                    find(i, 3)
                if y:
                    residual(i - 4)
                if w:
                    edge_weights(i - 3)
                if y and (i - 4) % GRP == GRP - 1:
                    norm_a((i - 4) // GRP)
                    norm_b((i - 4) // GRP)

            checked.wait(v, T - 1)
            V.tensor_reduce(badn[:], SQ[:], AX.X, ALU.add).then_inc(end_d, 1)
            v.wait_ge(end_d, 1)
            V.tensor_tensor(badm[:], badn[:], DEG[:], ALU.not_equal).then_inc(end_d, 1)
            v.wait_ge(end_d, 2)
            V.scalar_tensor_tensor(badn[:], ENDS[:], float(EDGES), badm[:], ALU.is_gt, ALU.max).then_inc(end_d, 1)
            v.wait_ge(end_d, 3)
            V.reduce_max(zs[:, 6:7], badn[:], AX.X).then_inc(end_d, 1)

            for t in range(T + 1):
                if t < T:
                    if t >= SLOTS:
                        y_ps.wait(v, t - SLOTS)
                    else:
                        zt_ps.wait(v, T - SLOTS + t)
                    edge_matrix(t, rt1)
                if t >= 1:
                    n = t - 1
                    o1_sb.wait(v, n)
                    if n >= 2:
                        v.wait_ge(stored[n % 2], 16 * (n // 2))
                    o_add.by(V.tensor_tensor(OT[:, n % 2, :], Y2[:, n % 2, :], X[:, n, :], ALU.add))
            v.wait_ge(end_p, 1)
            V.tensor_copy(flag[:], zs[:, 7:8]).then_inc(end_d, 1)
            v.wait_ge(end_d, 5)

        @block.scalar
        def _(a):
            S_ = nc.scalar

            for i in range(NGRP):
                ve0.wait(a, i)
                sq0.by(S_.activation(RT2[:, :, 0], VE[:, :, 0], ACT.Sqrt))
                negm0.wait(a, i)
                if i >= 2:
                    a.wait_ge(stored0[i % 2], 16 * (i // 2))
                for t in range(i * GRP, (i + 1) * GRP):
                    h0.by(S_.activation(HST[:, i % 2, t % GRP, :], X[:, t, :], ACT.Relu, bias=NEGM[:, t:t + 1], scale=RSTD[:, t:t + 1]))
                    if t >= 2:
                        g_keep(a, t - 2)
            g_keep(a, T - 2)
            g_keep(a, T - 1)
            a.wait_ge(z_dve, 3)
            S_.activation(NATT[:], G[:, :, D], ACT.Exp, bias=zs[:, 2:3], accum_out=zs[:, 3:4]).then_inc(z_act, 1)

            def squares(t, j):
                if j == 0:
                    a.wait_ge(in_a[t % ABUF], 16 * (t // ABUF + 1))
                if 2 * t + j >= 1:
                    a.wait_ge(checked.sem, 2 * t + j)
                n = NQ // 2
                checked.by(S_.activation(junk[:], A[:, t % ABUF, j * n:(j + 1) * n, 0:QC], ACT.Square, accum_out=SQ[:, t, j:j + 1]))

            def distance(t):
                negc.wait(a, t)
                if t >= 1:
                    rmat.wait(a, t - 1)
                dist.by(S_.activation(DIST[:], epos[:], ACT.Abs, bias=NEGC[:, t % SLOTS, :]))

            def exponent(t):
                snmax.wait(a, t)
                if t >= 1:
                    wrow.wait(a, t - 1)
                expd.by(S_.activation(EX[:], SR[:], ACT.Exp, bias=nmx[:], accum_out=es[:]))

            def weigh(t):
                wsum.wait(a, t)
                if t >= 2:
                    zt_ps.wait(a, t - 2)
                for c in range(CH):
                    ins = S_.activation(RW[:, t % 2, c, :], RT[:, t % SLOTS, c, :], ACT.Copy, scale=WE[:, t % SLOTS, c:c + 1])
                rw.by(ins)

            def keep_z(t):
                zt_ps.wait(a, t)
                if t >= 2:
                    o_ps.wait(a, t - 2)
                zt_sb.by(S_.copy(ZT[:, t % 2].rearrange("p c n -> p (c n)"), bZ[:, 0:D]))

            def next_h(t):
                if t % GRP == 0:
                    nm1.wait(a, t // GRP)
                h1.by(S_.activation(G[:, t, 0:D], X[:, t, :], ACT.Relu, bias=NEGM[:, t:t + 1], scale=RSTD[:, t:t + 1]))

            for i in range(T + 4):
                if 0 <= i - 4 < T:
                    weigh(i - 4)
                    keep_z(i - 4)
                if 0 <= i - 1 < T:
                    distance(i - 1)
                if i < T:
                    squares(i, 0)
                if 0 <= i - 3 < T:
                    exponent(i - 3)
                if i < T:
                    squares(i, 1)
                if 0 <= i - 4 < T and (i - 4) % GRP == GRP - 1:
                    ve1.wait(a, (i - 4) // GRP)
                    sq1.by(S_.activation(RT2[:], VE[:], ACT.Sqrt))
                if i - 4 - GRP >= 0:
                    next_h(i - 4 - GRP)
            for t in range(T - GRP, T):
                next_h(t)
            for t in range(T + 1):
                if t < T:
                    y_ps.wait(a, t)
                    if t >= 2:
                        o1_ps.wait(a, t - 2)
                    y_sb.by(S_.copy(ZT[:, t % 2].rearrange("p c n -> p (c n)"), (bZ, bW)[t % 2][:, 0:D]))
                if t >= 1:
                    n = t - 1
                    o1_ps.wait(a, n)
                    if n >= 2:
                        o_add.wait(a, n - 2)
                    o1_sb.by(S_.activation(Y2[:, n % 2, :], (bO, bI)[n % 2][:, 0:D], ACT.Relu, scale=DINV[:, n:n + 1]))

        @block.tensor
        def _(pe):
            MM = nc.tensor.matmul
            pe.wait_ge(c_dve, 4)
            pe.wait_ge(in_w, 80)
            for k in range(KC):
                for d in range(KC):
                    mm = nc.tensor.transpose(bW[:, d * D + k * P:d * D + (k + 1) * P], EW[:, k, d * P:(d + 1) * P], ident[:])
            mm.then_inc(ewt_ps, 1)
            pe.wait_ge(ewt_sb, 1)
            for k in range(KC):
                for d in range(KC):
                    mm = MM(bI[:, k * D:(k + 1) * D], EWT[:, d, k * P:(k + 1) * P], EWT[:, d, :], start=d == 0, stop=d == KC - 1)
            mm.then_inc(m_ps, 1)
            pe.wait_ge(m_sb, 1)

            def turn0(t):
                h0.wait(pe, t)
                if t >= 2:
                    ht0.wait(pe, t - 2)
                for c in range(KC):
                    mm = nc.tensor.transpose((bS, bW)[t % 2][:, c * P:(c + 1) * P], HST[:, t // GRP % 2, t % GRP, c * P:(c + 1) * P], ident[:])
                turned0.by(mm)

            def product0(t):
                ht0.wait(pe, t)
                if t >= 2:
                    g_sb.wait(pe, t - 2)
                for c in range(KC):
                    mm = MM((bO, bZ)[t % 2][:, 0:GW], RW[:, t % 2, c, :], MZ[:, c, :], start=c == 0, stop=c == KC - 1)
                g_ps.by(mm)

            for t in range(T + 1):
                if t < T:
                    turn0(t)
                if t >= 1:
                    product0(t - 1)
            g_sb.wait(pe, T - 1)
            pe.wait_ge(c_dve, 5)

            def g_edges(t, j):
                n = 3 * t + j
                if n >= 2:
                    v = n - 2
                    pe.wait_ge(score.sem, 5 * (v // 3) + min(2 * (v % 3) + 2, CH))
                for c in range(2 * j, min(2 * j + 2, CH)):
                    mm = MM(bG[n % 2][:, (c % 2) * D:(c % 2 + 1) * D], R[:, t % SLOTS, c * P:(c + 1) * P], G[:, t, 0:D], start=True, stop=True)
                gexp.by(mm)

            def prefixes(t):
                count.wait(pe, t)
                if t >= 1:
                    negc.wait(pe, t - 1)
                prefix.by(MM(bP[:, 0:1], below[:], CUM[:, t % SLOTS, L - 1:L], start=True, stop=True))

            def weighted(t):
                rw.wait(pe, t)
                if t >= 1:
                    zt_sb.wait(pe, t - 1)
                for d in range(KC):
                    for c in range(CH):
                        mm = MM(bZ[:, d * P:(d + 1) * P], HJ[:, t % SLOTS, c, d * P:(d + 1) * P], RW[:, t % 2, c, :], start=c == 0, stop=c == CH - 1)
                zt_ps.by(mm)

            def attended(t):
                zt_sb.wait(pe, t)
                if t >= 1:
                    x1.wait(pe, t - 1)
                for d in range(KC):
                    MM(bO[:, 0:D], ZT[:, t % 2, d, :], W0[:, d, :], start=d == 0, stop=False)
                o_ps.by(MM(bO[:, 0:D], ones_row[:], BIAS[:], start=False, stop=True))

            def by_row(t):
                scm.wait(pe, t)
                rtm.wait(pe, t)
                if t >= 1:
                    smask.wait(pe, t - 1)
                for c in range(CH):
                    mm = MM(bS[:, 0:L], RT[:, t % SLOTS, c, :], SM[:, t % SLOTS, c, :], start=c == 0, stop=c == CH - 1)
                srow.by(mm)

            def to_edges(t):
                rmat.wait(pe, t)
                if t >= 1:
                    jm.wait(pe, t - 1)
                place.wait(pe, t)
                K = 2 * L + 1
                for c in range(CH):
                    mm = MM(bI[:, c * K:(c + 1) * K], R[:, t % SLOTS, c * P:(c + 1) * P], LST[:, t % SLOTS, :], start=True, stop=True)
                listed.by(mm)

            def weights_edges(t):
                wrow.wait(pe, t)
                if t >= 1:
                    wm.wait(pe, t - 1)
                for c in range(CH):
                    mm = MM(bW[:, c * L:(c + 1) * L], R[:, t % SLOTS, c * P:(c + 1) * P], WR[:, t % SLOTS, :], start=True, stop=True)
                wed.by(mm)

            pe.wait_ge(c_dve, 5 + SLOTS)
            for i in range(T + 4):
                u, w, y = 0 <= i - 1 < T, 0 <= i - 3 < T, 0 <= i - 4 < T
                if w:
                    g_edges(i - 3, 0)
                    g_edges(i - 3, 1)
                if u:
                    prefixes(i - 1)
                if y:
                    weighted(i - 4)
                if w:
                    g_edges(i - 3, 2)
                if y:
                    attended(i - 4)
                if w:
                    by_row(i - 3)
                if u:
                    to_edges(i - 1)
                if w:
                    weights_edges(i - 3)

            def gathered_sum(t):
                s = t % SLOTS
                pe.wait_ge(g1[s], 16 * CH * (t // SLOTS + 1))
                rt1.wait(pe, t)
                if t >= 2:
                    y_sb.wait(pe, t - 2)
                b = (bZ, bW)[t % 2]
                for d in range(KC):
                    MM(b[:, d * P:(d + 1) * P], G[:, t, d * P:(d + 1) * P], ident[:], start=True, stop=False)
                    for c in range(CH):
                        mm = MM(b[:, d * P:(d + 1) * P], HJ[:, s, c, d * P:(d + 1) * P], RT[:, s, c, :], start=False, stop=c == CH - 1)
                y_ps.by(mm)

            def convolved(t):
                y_sb.wait(pe, t)
                if t >= 2:
                    o1_sb.wait(pe, t - 2)
                for d in range(KC):
                    mm = MM((bO, bI)[t % 2][:, 0:D], ZT[:, t % 2, d, :], W1[:, d, :], start=d == 0, stop=d == KC - 1)
                o1_ps.by(mm)

            h1.wait(pe, T - 1)
            for t in range(T + 1):
                if t < T:
                    gathered_sum(t)
                if t >= 1:
                    convolved(t - 1)


class Chain:

    def __init__(self, sem, per=0, base=0):
        self.sem, self.per, self.base, self.n = sem, per, base, 0

    def done(self, ins):
        self.n += 1
        ins.then_inc(self.sem, 1)

    def at(self, turn, k):
        return turn * self.per + (self.base + k)

    def link(self, eng, turn, ins):
        self.done(ins)
        eng.wait_ge(self.sem, self.at(turn, self.n))


def general_path(nc, flag, x, adj, w0, bias, node_w, edge_w, w1, out, table):
    adj_t = adj.rearrange("(t p) n -> t p n", p=P)
    table_t = table.rearrange("(t p) d -> t p d", p=P)
    out_t = out.rearrange("(t p) d -> t p d", p=P)
    with ExitStack() as ctx:
        def sb(name, shape, dt=F32):
            return ctx.enter_context(nc.sbuf_tensor("general_" + name, shape, dt))

        def ps(name):
            return ctx.enter_context(nc.psum_tensor("general_" + name, [P, SC], F32))

        def sem(name):
            return ctx.enter_context(nc.semaphore(name))

        X = sb("X", [P, T, D])
        QT = sb("QT", [P, KC, N])
        SUP = sb("SUP", [P, T, D])
        AT = sb("AT", [P, N])
        S = sb("S", [P, N])
        PT = sb("PT", [P, 2, SC])
        W0 = sb("W0", [P, KC, D])
        EW = sb("EW", [P, KC, D])
        W1 = sb("W1", [P, KC, D])
        NW = sb("NW", [P, KC])
        BIAS = sb("BIAS", [P, D])
        ident = sb("ident", [P, P])
        xc = sb("xc", [P, D])
        hn = sb("hn", [P, D])
        hT = sb("hT", [P, KC, P])
        qs = sb("qs", [P, KC, P])
        tmp = sb("tmp", [P, SC])
        Z = sb("Z", [P, T])
        NATT = sb("NATT", [P, T])
        DI = sb("DI", [P, T])
        sm = sb("sm", [P, 16])
        c1 = lambda i: sm[:, i:i + 1]
        psS = [ps(f"psS{i}") for i in range(2)]
        psT = [ps(f"psT{i}") for i in range(2)]
        psQ, psO, psZ = ps("psQ"), ps("psO"), ps("psZ")

        g_in = sem("g_inputs")
        g_adj = sem("g_adj")
        g_id = sem("g_identity")
        g_tab = sem("g_table")
        g_back = sem("g_table_back")
        g_out = sem("g_out")
        g_pool = sem("g_pool")
        dsem = [sem(f"g_dve{i}") for i in range(4)]
        asem = [sem(f"g_act{i}") for i in range(4)]
        psem = [sem(f"g_pe{i}") for i in range(4)]
        D1, D2, D3 = 10, 45, 3
        A1, A2, A3 = 3, 11, 9
        P1, P2, P3 = 2, 17, 18
        block = ctx.enter_context(nc.Block())

        def layernorm(v, ch, t, src, act_sem, act_at):
            ch.link(v, t, nc.vector.tensor_scalar_mul(xc[:], src, 1.0))
            ch.link(v, t, nc.vector.reduce_sum(c1(0), xc[:], AX.X))
            ch.link(v, t, nc.vector.tensor_scalar_mul(c1(1), c1(0), -1.0 / D))
            ch.link(v, t, nc.vector.tensor_scalar_add(xc[:], xc[:], c1(1)))
            ch.link(v, t, nc.vector.tensor_tensor_reduce(out=tmp[:, 0:D], in0=xc[:], in1=xc[:], scale=1.0, scalar=0.0,
                                                         op0=ALU.mult, op1=ALU.add, accum_out=c1(2)))
            ch.link(v, t, nc.vector.tensor_scalar(c1(3), c1(2), 1.0 / D, EPS, ALU.mult, ALU.add))
            v.wait_ge(act_sem, act_at)
            ch.link(v, t, nc.vector.reciprocal(c1(5), c1(4)))
            ch.link(v, t, nc.vector.tensor_scalar(hn[:], xc[:], c1(5), 0.0, ALU.mult, ALU.max))

        @block.sync
        def _(sp):
            wanted = sp.value_load(flag[0:1, 0:1])
            with sp.If(wanted > 0):
                sp.sem_inc(dsem[2], D2)
                sp.sem_inc(psem[3], P3)
                sp.sem_inc(asem[3], A3)
                sp.sem_inc(g_tab, 16)
                sp.sem_inc(g_out, 16)
                sp.dma_start(X[:], x.rearrange("(t p) d -> p t d", p=P)).then_inc(g_in, 16)
                for dst, src in ((W0, w0), (EW, edge_w), (W1, w1)):
                    sp.dma_start(dst[:], src.rearrange("(c p) n -> p c n", p=P)).then_inc(g_in, 16)
                with nc.allow_non_contiguous_dma(reason="256 values of the node weights"):
                    sp.dma_start(NW[:], node_w.rearrange("(c p) o -> p (c o)", p=P)).then_inc(g_in, 16)
                sp.dma_start(BIAS[:], bias.rearrange("(o n) -> o n", o=1).broadcast_to([P, D])).then_inc(g_in, 16)
                with sp.Fori(0, T) as t:
                    sp.wait_ge(dsem[2], t * D2 + D2)
                    sp.dma_start(AT[:], adj_t[t]).then_inc(g_adj, 16)
                    sp.wait_ge(dsem[2], t * D2 + D2 + D2)
                    sp.dma_start(table_t[t], hn[:]).then_inc(g_tab, 16)
                sp.wait_ge(g_tab, 16 * (T + 1))
                sp.wait_ge(psem[2], T * P2)
                sp.dma_start(SUP[:], table.rearrange("(t p) d -> p t d", p=P)).then_inc(g_back, 16)
                with sp.Fori(0, T) as t:
                    sp.wait_ge(psem[3], t * P3 + P3)
                    sp.dma_start(AT[:], adj_t[t]).then_inc(g_adj, 16)
                    sp.wait_ge(dsem[3], t * D3 + D3)
                    sp.dma_start(out_t[t], hn[:]).then_inc(g_out, 16)
                sp.wait_ge(g_out, 16 * (T + 1))
            sp.nop()

        @block.gpsimd
        def _(g):
            wanted = g.value_load(flag[0:1, 0:1])
            with g.If(wanted > 0):
                g.memset(ident[:], 0.0).then_inc(g_id, 1)
                g.wait_ge(g_id, 1)
                g.affine_select(out=ident[:], in_=ident[:], compare_op=ALU.not_equal, fill=1.0, base=0,
                                pattern=[[-1, P]], channel_multiplier=1).then_inc(g_id, 1)
                g.wait_ge(dsem[1], 1)
                g.partition_all_reduce(c1(7), c1(6), P, bass.bass_isa.ReduceOp.max).then_inc(g_pool, 1)
                g.wait_ge(asem[1], 1)
                g.partition_all_reduce(c1(10), c1(9), P, bass.bass_isa.ReduceOp.add).then_inc(g_pool, 1)
            g.nop()

        @block.vector
        def _(v):
            wanted = v.value_load(flag[0:1, 0:1])
            with v.If(wanted > 0):
                v.wait_ge(g_in, 96)
                ch = Chain(dsem[0], D1)
                with v.Fori(0, T) as t:
                    ch.n = 0
                    layernorm(v, ch, t, X[:, t, :], asem[0], t * A1 + 1)
                    v.wait_ge(psem[0], t * P1 + 2)
                    ch.done(nc.vector.tensor_copy(SUP[:, t, :], psO[:, 0:D]))
                    ch.link(v, t, nc.vector.tensor_copy(Z[:, bass.ds(t, 1)], psZ[:, 0:1]))
                    assert ch.n == D1
                ch = Chain(dsem[1])
                ch.link(v, 0, nc.vector.reduce_max(c1(6), Z[:], AX.X))
                v.wait_ge(g_pool, 1)
                ch.link(v, 0, nc.vector.tensor_scalar_mul(c1(8), c1(7), -1.0))
                v.wait_ge(g_pool, 2)
                ch.link(v, 0, nc.vector.reciprocal(c1(11), c1(10)))
                v.wait_ge(asem[1], 1)
                ch.link(v, 0, nc.vector.tensor_scalar_mul(NATT[:], NATT[:], c1(11)))

                ch = Chain(dsem[2], D2, D2)
                with v.Fori(0, T) as t:
                    ch.n = 0
                    v.wait_ge(g_adj, t * 16 + 16)
                    ch.done(nc.vector.tensor_copy(qs[:], QT[:, :, bass.ds(t * P, P)]))
                    ch.link(v, t, nc.vector.reduce_sum(c1(12), AT[:], AX.X))
                    for c in range(NS):
                        cs = slice(c * SC, (c + 1) * SC)
                        ch.link(v, t, nc.vector.tensor_scalar(tmp[:], AT[:, cs], 0.0, -NEG_BIG, ALU.is_gt, ALU.mult))
                        v.wait_ge(psem[2], t * P2 + c + 1)
                        ch.link(v, t, nc.vector.scalar_tensor_tensor(S[:, cs], AT[:, cs], 0.0, psS[c % 2][:], ALU.is_gt, ALU.mult))
                        ch.link(v, t, nc.vector.scalar_tensor_tensor(S[:, cs], tmp[:], NEG_BIG, S[:, cs], ALU.add, ALU.add))
                    ch.link(v, t, nc.vector.reduce_max(c1(6), S[:], AX.X))
                    ch.link(v, t, nc.vector.tensor_scalar_mul(c1(8), c1(6), -1.0))
                    v.wait_ge(asem[2], t * A2 + 1)
                    ch.link(v, t, nc.vector.tensor_tensor(S[:], S[:], AT[:], ALU.mult))
                    ch.link(v, t, nc.vector.reciprocal(c1(10), c1(9)))
                    ch.link(v, t, nc.vector.tensor_tensor(c1(11), c1(10), NATT[:, bass.ds(t, 1)], ALU.mult))
                    v.wait_ge(psem[2], t * P2 + P2)
                    ch.link(v, t, nc.vector.scalar_tensor_tensor(tmp[:, 0:D], psO[:, 0:D], c1(11), BIAS[:], ALU.mult, ALU.add))
                    ch.link(v, t, nc.vector.tensor_tensor(X[:, t, :], X[:, t, :], tmp[:, 0:D], ALU.add))
                    v.wait_ge(g_tab, t * 16 + 16)
                    layernorm(v, ch, t, X[:, t, :], asem[2], t * A2 + 10)
                    ch.link(v, t, nc.vector.tensor_scalar_add(c1(13), c1(12), 1.0))
                    v.wait_ge(asem[2], t * A2 + 11)
                    ch.link(v, t, nc.vector.reciprocal(c1(15), c1(14)))
                    ch.done(nc.vector.tensor_copy(DI[:, bass.ds(t, 1)], c1(15)))
                    ch.link(v, t, nc.vector.tensor_scalar_mul(hn[:], hn[:], c1(15)))
                    assert ch.n == D2, ch.n

                ch = Chain(dsem[3], D3)
                v.wait_ge(g_back, 16)
                v.wait_ge(g_tab, 16 * (T + 1))
                with v.Fori(0, T) as t:
                    ch.n = 0
                    v.wait_ge(psem[3], t * P3 + P3 + 16)
                    ch.link(v, t, nc.vector.tensor_tensor(xc[:], psO[:, 0:D], SUP[:, t, :], ALU.add))
                    ch.link(v, t, nc.vector.tensor_scalar_mul(xc[:], xc[:], DI[:, bass.ds(t, 1)]))
                    v.wait_ge(psem[3], t * P3 + P3 + P3)
                    v.wait_ge(g_out, t * 16 + 16)
                    ch.link(v, t, nc.vector.scalar_tensor_tensor(hn[:], psQ[:, 0:D], 0.0, X[:, t, :], ALU.max, ALU.add))
                    assert ch.n == D3, ch.n
            v.nop()

        @block.scalar
        def _(a):
            wanted = a.value_load(flag[0:1, 0:1])
            with a.If(wanted > 0):
                with a.Fori(0, T) as t:
                    a.wait_ge(dsem[0], t * D1 + 6)
                    nc.scalar.activation(c1(4), c1(3), ACT.Sqrt).then_inc(asem[0], 1)
                    a.wait_ge(psem[0], t * P1 + 1)
                    nc.scalar.copy(hT[:].rearrange("p c n -> p (c n)"), psT[0][:, 0:D]).then_inc(asem[0], 1)
                    a.wait_ge(psem[0], t * P1 + 2)
                    nc.scalar.copy(QT[:, :, bass.ds(t * P, P)], psQ[:, 0:D].rearrange("p (c n) -> p c n", c=KC)).then_inc(asem[0], 1)
                a.wait_ge(dsem[1], 2)
                nc.scalar.activation(NATT[:], Z[:], ACT.Exp, bias=c1(8), accum_out=c1(9)).then_inc(asem[1], 1)
                with a.Fori(0, T) as t:
                    a.wait_ge(dsem[2], t * D2 + D2 + 28)
                    nc.scalar.activation(S[:], S[:], ACT.Exp, bias=c1(8), accum_out=c1(9)).then_inc(asem[2], 1)
                    for g in range(NS):
                        a.wait_ge(psem[2], t * P2 + 8 + g + 1)
                        nc.scalar.copy(PT[:, g % 2, :], psT[g % 2][:]).then_inc(asem[2], 1)
                    a.wait_ge(dsem[2], t * D2 + D2 + 39)
                    nc.scalar.activation(c1(4), c1(3), ACT.Sqrt).then_inc(asem[2], 1)
                    a.wait_ge(dsem[2], t * D2 + D2 + 42)
                    nc.scalar.activation(c1(14), c1(13), ACT.Sqrt).then_inc(asem[2], 1)
                with a.Fori(0, T) as t:
                    for g in range(NS):
                        a.wait_ge(psem[3], t * P3 + P3 + g + 1 + (g > 0) * (g - 1))
                        nc.scalar.copy(PT[:, g % 2, :], psT[g % 2][:]).then_inc(asem[3], 1)
                    a.wait_ge(psem[3], t * P3 + P3 + 17)
                    nc.scalar.copy(hT[:].rearrange("p c n -> p (c n)"), psT[0][:, 0:D]).then_inc(asem[3], 1)
            a.nop()

        @block.tensor
        def _(pe):
            wanted = pe.value_load(flag[0:1, 0:1])
            with pe.If(wanted > 0):
                pe.wait_ge(g_id, 2)
                pe.wait_ge(g_in, 96)

                def turn(src):
                    for c in range(KC):
                        mm = nc.tensor.transpose(psT[0][:, c * P:(c + 1) * P], src[:, c * P:(c + 1) * P], ident[:])
                    return mm

                with pe.Fori(0, T) as t:
                    pe.wait_ge(dsem[0], t * D1 + 8)
                    turn(hn).then_inc(psem[0], 1)
                    pe.wait_ge(asem[0], t * A1 + 2)
                    for d in range(KC):
                        for c in range(KC):
                            nc.tensor.matmul(psQ[:, d * P:(d + 1) * P], EW[:, c, d * P:(d + 1) * P], hT[:, c, :], start=c == 0, stop=c == KC - 1)
                    for c in range(KC):
                        nc.tensor.matmul(psO[:, 0:D], hT[:, c, :], W0[:, c, :], start=c == 0, stop=c == KC - 1)
                    for c in range(KC):
                        mm = nc.tensor.matmul(psZ[:, 0:1], hT[:, c, :], NW[:, c:c + 1], start=c == 0, stop=c == KC - 1)
                    mm.then_inc(psem[0], 1)
                    pe.wait_ge(asem[0], t * A1 + 3)

                def transposes(src, g):
                    for k in range(SC // P):
                        b = g * (SC // P) + k
                        mm = nc.tensor.transpose(psT[g % 2][:, k * P:(k + 1) * P], src[:, b * P:(b + 1) * P], ident[:])
                    return mm

                def products(g):
                    for k in range(SC // P):
                        b = g * (SC // P) + k
                        mm = nc.tensor.matmul(psO[:, 0:D], PT[:, g % 2, k * P:(k + 1) * P], SUP[:, b, :], start=b == 0, stop=b == T - 1)
                    return mm

                pe.wait_ge(dsem[0], T * D1)
                with pe.Fori(0, T) as t:
                    pe.wait_ge(dsem[2], t * D2 + D2 + 2)
                    for c in range(NS):
                        if c >= 2:
                            pe.wait_ge(dsem[2], t * D2 + D2 + 2 + 3 * (c - 2) + 2)
                        for k in range(KC):
                            mm = nc.tensor.matmul(psS[c % 2][:], qs[:, k, :], QT[:, k, c * SC:(c + 1) * SC], start=k == 0, stop=k == KC - 1)
                        mm.then_inc(psem[2], 1)
                    pe.wait_ge(dsem[2], t * D2 + D2 + 29)
                    transposes(S, 0).then_inc(psem[2], 1)
                    for g in range(NS):
                        if g + 1 < NS:
                            if g >= 1:
                                pe.wait_ge(asem[2], t * A2 + 1 + g)
                            transposes(S, g + 1).then_inc(psem[2], 1)
                        pe.wait_ge(asem[2], t * A2 + 1 + g + 1)
                        mm = products(g)
                    mm.then_inc(psem[2], 1)
                pe.wait_ge(g_back, 16)
                with pe.Fori(0, T) as t:
                    pe.wait_ge(g_adj, t * 16 + 16 * (T + 1))
                    pe.wait_ge(asem[3], t * A3 + A3)
                    transposes(AT, 0).then_inc(psem[3], 1)
                    for g in range(NS):
                        if g + 1 < NS:
                            if g >= 1:
                                pe.wait_ge(asem[3], t * A3 + A3 + g)
                            transposes(AT, g + 1).then_inc(psem[3], 1)
                        pe.wait_ge(asem[3], t * A3 + A3 + g + 1)
                        products(g).then_inc(psem[3], 1)
                    pe.wait_ge(dsem[3], t * D3 + 2)
                    turn(xc).then_inc(psem[3], 1)
                    pe.wait_ge(asem[3], t * A3 + A3 + 9)
                    for c in range(KC):
                        mm = nc.tensor.matmul(psQ[:, 0:D], hT[:, c, :], W1[:, c, :], start=c == 0, stop=c == KC - 1)
                    mm.then_inc(psem[3], 1)
                    pe.wait_ge(dsem[3], t * D3 + 3)
            pe.nop()


def build(nc, x, adj, w0, bias, node_w, edge_w, w1, out):
    with nc.sbuf_tensor("flag", [P, 1], I32) as flag:
        table0 = nc.dram_tensor("h0_rows", [N, D], F32, kind="Internal").ap()
        table1 = nc.dram_tensor("h1_rows", [N, D], F32, kind="Internal").ap()
        edge_path(nc, flag, x, adj, w0, bias, node_w, edge_w, w1, out, table0, table1)
        general_path(nc, flag, x, adj, w0, bias, node_w, edge_w, w1, out, table1)


_INS = ["x", "adj", "L0_gnn_weight", "L0_gnn_bias", "L0_gnn_node_w", "L0_gnn_edge_w", "L1_gnn_W"]


def kernel(**inputs):
    import numpy as _np
    import concourse.bacc as _bacc
    from concourse import mybir as _mybir
    from concourse.bass_utils import run_bass_kernel_spmd as _run

    nc = _bacc.Bacc("TRN2", target_bir_lowering=False, num_devices=1)
    arrays, args = {}, []
    for name in _INS:
        a = _np.ascontiguousarray(inputs[name])
        arrays[f"in_{name}_dram"] = a
        args.append(nc.dram_tensor(f"in_{name}_dram", a.shape, _mybir.dt.from_np(a.dtype), kind="ExternalInput").ap())
    args.append(nc.dram_tensor("out_0_dram", (N, D), _mybir.dt.float32, kind="ExternalOutput").ap())
    build(nc, *args)
    r = _run(nc, [arrays], core_ids=[0])
    return r.results[0]["out_0_dram"]
```

```python
from contextlib import ExitStack

import concourse.bass as bass
from concourse import mybir

F32 = mybir.dt.float32
BF16 = mybir.dt.bfloat16
I32 = mybir.dt.int32
U32 = mybir.dt.uint32
ALU = mybir.AluOpType
ACT = mybir.ActivationFunctionType
AX = mybir.AxisListType

P = 128
N = 4096
D = 256
T = N // P
KC = D // P
SC = 512
NS = N // SC
NEG_BIG = -9000000000000000.0
EPS = 1e-5


RMAX = bass.bass_isa.ReduceOp.max
RADD = bass.bass_isa.ReduceOp.add

NQ = 4
QC = N // NQ
SEG_CAP = 8
L = NQ * SEG_CAP
CH = 5
EDGES = CH * P
NONE = 2 * N
SLOTS = 4
LSLOTS = 8
LEAD = 4
ABUF = 3
GRP = 8
GROUPS = [(0, 8), (8, 16), (16, 24), (24, 30), (30, 32)]
GW = D + 1


class Signal:

    def __init__(self, sem, per=1):
        self.sem, self.per = sem, per

    def by(self, ins):
        return ins.then_inc(self.sem, 1)

    def wait(self, eng, t, k=None):
        eng.wait_ge(self.sem, t * self.per + (self.per if k is None else k))


def edge_path(nc, flag, x, adj, w0, bias, node_w, edge_w, w1, out, table0, table1):
    adj_q = adj.rearrange("(t p) (q c) -> t p q c", p=P, q=NQ)
    x_t = x.rearrange("(t p) d -> p t d", p=P)
    t0_t = table0.rearrange("(t p) d -> p t d", p=P)
    t1_t = table1.rearrange("(t p) d -> p t d", p=P)
    out_t = out.rearrange("(t p) d -> t p d", p=P)
    ctx = ExitStack()
    with ctx:
        def sb(name, shape, dt=F32):
            return ctx.enter_context(nc.sbuf_tensor(name, shape, dt))

        def bank(name):
            return ctx.enter_context(nc.psum_tensor(name, [P, SC], F32))

        def sem(name):
            return ctx.enter_context(nc.semaphore(name))

        def sig(name, per=1):
            return Signal(sem(name), per)

        X = sb("X", [P, T, D])
        G = sb("G", [P, T, GW])
        A = sb("A", [P, ABUF, NQ, QC + SEG_CAP])
        NBR = sb("NBR", [P, T, CH], U32)
        ROW = sb("ROW", [P, T, CH])
        CUM = sb("CUM", [P, T, L])
        DEG = CUM[:, :, L - 1]
        HALF = sb("HALF", [P, T])
        NEGC = sb("NEGC", [P, T])
        SQ = sb("SQ", [P, T, 2])
        NATT = sb("NATT", [P, T])
        MV = sb("MV", [P, T, 2])
        VE = sb("VE", [P, GRP, 2])
        RT2 = sb("RT2", [P, GRP, 2])
        RSTD = sb("RSTD", [P, T])
        NEGM = sb("NEGM", [P, T])
        DINV = sb("DINV", [P, T])
        MZ = sb("MZ", [P, KC, GW])
        EW = sb("EW", [P, KC, D])
        EWT = sb("EWT", [P, KC, D])
        W0 = sb("W0", [P, KC, D])
        W1 = sb("W1", [P, KC, D])
        BIAS = sb("BIAS", [1, D])
        ones_row = sb("ones_row", [1, P])
        ones8 = sb("ones8", [P, SEG_CAP])
        col1 = sb("col1", [P, P])
        par1 = sb("par1", [P, 1])
        ident = sb("ident", [P, P])
        below = sb("below", [P, P])
        epos = sb("epos", [P, EDGES])
        eown = sb("eown", [P, CH, L])
        nbase = sb("nbase", [P, NQ, SEG_CAP])
        IDX = sb("IDX", [P, LSLOTS, NQ, SEG_CAP], U32)
        VAL = sb("VAL", [P, LSLOTS, L])
        LST = sb("LST", [P, SLOTS, 2 * L + 1])
        DIST = sb("DIST", [P, EDGES])
        R = sb("R", [P, SLOTS, EDGES])
        RT = sb("RT", [P, SLOTS, CH, P])
        RW = sb("RW", [P, 2, CH, P])
        HJ = sb("HJ", [P, SLOTS, CH, D])
        MAT = sb("MAT", [P, SLOTS, CH, L])
        tl = sb("tl", [P, CH, L])
        js = sb("js", [P, CH])
        prod = sb("prod", [P, 2, D])
        sc = sb("sc", [P, SLOTS, CH])
        SM = sb("SM", [P, SLOTS, CH, L])
        DF = sb("DF", [P, CH])
        EE = sb("EE", [P, CH])
        WE = sb("WE", [P, SLOTS, CH])
        PEN = sb("PEN", [P, SLOTS, L])
        SR = sb("SR", [P, L])
        EX = sb("EX", [P, L])
        MS = sb("MS", [P, SLOTS, 2])
        es = sb("es", [P, 1])
        rs = sb("rs", [P, 1])
        ZT = sb("ZT", [P, 2, KC, P])
        st = sb("st", [P, 2, 6])
        HST = HJ[:].rearrange("p s c d -> p (s c d)")[:, 0:2 * GRP * D].rearrange("p (b t d) -> p b t d", b=2, t=GRP)
        junk = sb("junk", [P, NQ // 2, QC], BF16)
        Y2 = sb("Y2", [P, 2, D])
        OT = sb("OT", [P, 2, D])
        zs = sb("zs", [P, 8])
        badm = sb("badm", [P, T])
        badn = sb("badn", [P, T])

        bI, bS, bZ, bO, bR = (bank(f"bank{i}") for i in range(5))
        bG = [bank(f"bank{i}") for i in range(5, 8)]
        PFX, SCR, MSE = bS[:, 0:1], bR[:, 0:L], bR[:, 128:128 + 2 * CH]

        in_e = sem("edge_w_in")
        in_w = sem("weights_in")
        in_x = [sem(f"x_in{i}") for i in range(T // GRP)]
        in_a = [sem(f"adj_in{i}") for i in range(ABUF)]
        c_pool = sem("pool_constants")
        c_dve = sem("dve_constants")
        c_mem = sem("slots_cleared")
        ewt_ps, ewt_sb, m_ps, m_sb = (sem(n) for n in ("edge_w_turned", "edge_w_T_kept", "m_product", "m_kept"))
        stat0, aggr0 = sig("stats0"), sig("means0")
        ve0, sq0, rstd0, negm0 = (sig(n) for n in ("var0", "root0", "rstd0", "negmean0"))
        h0, turned0, ht0, g_ps, g_sb = (sig(n) for n in ("h0", "h0_turned", "h0T_kept", "g_product", "g_kept"))
        stored0 = [sem(f"table0_stored{i}") for i in range(2)]
        z_dve, z_pool, z_act = sem("node_dve"), sem("node_pool"), sem("node_act")
        found, checked = sig("found", NQ), sig("squares_summed", 2)
        valid, node, count, prefix = sig("valid"), sig("node_listed"), sig("counted"), sig("prefix")
        place, half, negc, dist, rmat = sig("placed"), sig("half"), sig("negcentre"), sig("distance"), sig("rows_matrix")
        listed, match, jm, jr, nbr, row = (sig(n) for n in ("listed", "match", "nbr_masked", "nbr_summed", "nbr", "edge_row"))
        gath = [sem(f"gathered{i}") for i in range(SLOTS)]
        rtm = sig("edge_matrix")
        gexp = sig("g_at_edges", 3)
        score, scm = sig("scores", CH), sig("scores_placed")
        srow, smask, smax = sig("scores_by_row"), sig("scores_masked"), sig("row_max")
        expd, inv, rscale = sig("exponentials"), sig("row_inverse"), sig("row_scale")
        msed, diff, eexp, wedge, rw = sig("scale_at_edges"), sig("edge_difference"), sig("edge_exp"), sig("edge_weight"), sig("weighted_matrix")
        zt_ps, zt_sb, o_ps, x1, stat1, aggr1 = (sig(n) for n in ("z_product", "z_kept", "o_product", "x1", "stats1", "means1"))
        ve1, sq1, inv1, rd1, nm1 = (sig(n) for n in ("var1", "root1", "inverse1", "scale1", "negmean1"))
        h1 = sig("h1")
        stored1 = sem("table1_stored")
        end_d, end_p = sem("flag_dve"), sem("flag_pool")
        g1 = [sem(f"gathered_again{i}") for i in range(SLOTS)]
        rt1, y_ps, y_sb, o1_ps, o1_sb, o_add = (sig(n) for n in ("edge_matrix1", "y_product", "y_kept", "o1_product", "o1_kept", "o1_added"))
        stored = [sem(f"out_stored{i}") for i in range(2)]
        NGRP = T // GRP
        block = ctx.enter_context(nc.Block())

        def keep1(sp, i):
            a, b = GROUPS[i]
            h1.wait(sp, b - 1)
            sp.dma_start(t1_t[:, a:b, :], G[:, a:b, 0:D]).then_inc(stored1, 16)

        def g_keep(a, t):
            g_ps.wait(a, t)
            g_sb.by(nc.scalar.copy(G[:, t, :], (bO, bZ, bR, bG[2])[t % 4][:, 0:GW]))

        @block.sync
        def _(sp):
            sp.dma_start(EW[:], edge_w.rearrange("(c p) n -> p c n", p=P)).then_inc(in_e, 16)
            for i in range(NGRP):
                g = slice(i * GRP, (i + 1) * GRP)
                sp.dma_start(X[:, g, :], x_t[:, g, :]).then_inc(in_x[i], 16)
                if i == 0:
                    for dst, src in ((W0, w0), (W1, w1)):
                        sp.dma_start(dst[:], src.rearrange("(c p) n -> p c n", p=P)).then_inc(in_w, 16)
                    with nc.allow_non_contiguous_dma(reason="256 values of the node weights"):
                        sp.dma_start(MZ[:, :, D:GW], node_w.rearrange("(c p) o -> p c o", p=P)).then_inc(in_w, 16)
                    sp.dma_start(BIAS[:], bias.rearrange("(o n) -> o n", o=1)).then_inc(in_w, 16)

            def load(t):
                if t >= ABUF:
                    found.wait(sp, t - ABUF)
                    checked.wait(sp, t - ABUF)
                sp.dma_start(A[:, t % ABUF, :, 0:QC], adj_q[t]).then_inc(in_a[t % ABUF], 16)

            for t in range(ABUF):
                load(t)
            for i in range(NGRP):
                h0.wait(sp, (i + 1) * GRP - 1)
                sp.dma_start(t0_t[:, i * GRP:(i + 1) * GRP, :], HST[:, i % 2]).then_inc(stored0[i % 2], 16)
                if i > 0:
                    load(ABUF + i - 1)
            for t in range(ABUF + NGRP - 1, T):
                load(t)
                if t == 28:
                    keep1(sp, 0)
            for i in range(1, len(GROUPS)):
                keep1(sp, i)
            for t in range(T):
                o_add.wait(sp, t)
                sp.dma_start(out_t[t], OT[:, t % 2, :]).then_inc(stored[t % 2], 16)
            for s in stored:
                sp.wait_ge(s, 16 * (T // 2))

        @block.gpsimd
        def _(g):
            f = dict(allow_small_or_imprecise_dtypes=True)
            g.iota(col1[:], pattern=[[1, P]], base=1, channel_multiplier=0, **f).then_inc(c_pool, 1)
            g.iota(par1[:], pattern=[[0, 1]], base=1, channel_multiplier=1, **f).then_inc(c_pool, 1)
            g.iota(epos[:], pattern=[[1, EDGES]], base=0, channel_multiplier=0, **f).then_inc(c_pool, 1)
            g.iota(eown[:], pattern=[[P, CH], [0, L]], base=1, channel_multiplier=1, **f).then_inc(c_pool, 1)
            g.iota(nbase[:], pattern=[[-QC, NQ], [0, SEG_CAP]], base=NONE, channel_multiplier=0, **f).then_inc(c_pool, 1)
            g.wait_ge(z_dve, 2)
            g.partition_all_reduce(zs[:, 1:2], zs[:, 0:1], P, RMAX).then_inc(z_pool, 1)
            g.wait_ge(z_act, 1)
            g.partition_all_reduce(zs[:, 4:5], zs[:, 3:4], P, RADD).then_inc(z_pool, 1)
            for s in stored0:
                g.wait_ge(s, 16 * (NGRP // 2))
            turned0.wait(g, T - 1)
            g.memset(HJ[:], 0.0).then_inc(c_mem, 1)
            g.wait_ge(c_mem, 1)
            for t in range(T):
                nbr.wait(g, t)
                if t >= SLOTS:
                    zt_ps.wait(g, t - SLOTS)
                for c in range(CH):
                    g.indirect_dma_start(out=HJ[:, t % SLOTS, c, :], out_offset=None, in_=table0,
                                         in_offset=bass.IndirectOffsetOnAxis(ap=NBR[:, t, c:c + 1], axis=0),
                                         bounds_check=N - 1, oob_is_err=False).then_inc(gath[t % SLOTS], 16)
            g.wait_ge(stored1, 16 * len(GROUPS))
            for t in range(T):
                if t < SLOTS:
                    zt_ps.wait(g, T - SLOTS + t)
                else:
                    y_ps.wait(g, t - SLOTS)
                for c in range(CH):
                    g.indirect_dma_start(out=HJ[:, t % SLOTS, c, :], out_offset=None, in_=table1,
                                         in_offset=bass.IndirectOffsetOnAxis(ap=NBR[:, t, c:c + 1], axis=0),
                                         bounds_check=N - 1, oob_is_err=False).then_inc(g1[t % SLOTS], 16)
            g.wait_ge(end_d, 5)
            g.partition_all_reduce(zs[:, 7:8], zs[:, 6:7], P, RMAX).then_inc(end_p, 1)

        @block.vector
        def _(v):
            V = nc.vector
            V.memset(ones8[:], 1.0).then_inc(c_dve, 1)
            V.memset(A[:, :, :, QC:], 1.0).then_inc(c_dve, 1)
            V.memset(ones_row[:], 1.0).then_inc(c_dve, 1)
            v.wait_ge(c_pool, 5)
            V.tensor_scalar(ident[:], col1[:], par1[:], None, ALU.is_equal).then_inc(c_dve, 1)
            V.tensor_scalar(below[:], col1[:], par1[:], None, ALU.is_gt).then_inc(c_dve, 1)
            for s in range(SLOTS):
                V.tensor_copy(LST[:, s, 2 * L:], par1[:]).then_inc(c_dve, 1)
            v.wait_ge(ewt_ps, 1)
            V.tensor_copy(EWT[:].rearrange("p c n -> p (c n)"), bZ[:]).then_inc(ewt_sb, 1)
            v.wait_ge(m_ps, 1)
            V.tensor_copy(MZ[:, :, 0:D], bI[:].rearrange("p (c n) -> p c n", c=KC)).then_inc(m_sb, 1)

            def v_stat(t):
                if t % GRP == 0:
                    v.wait_ge(in_x[t // GRP], 16)
                stat0.by(V.bn_stats(st[:, t % 2, :], X[:, t, :]))
                stat0.wait(v, t)
                aggr0.by(V.bn_aggr(MV[:, t, :], st[:, t % 2, :]))

            def roots0(i):
                gs = slice(i * GRP, (i + 1) * GRP)
                aggr0.wait(v, (i + 1) * GRP - 1)
                ve0.by(V.tensor_scalar_add(VE[:, :, 0], MV[:, gs, 1], EPS))
                sq0.wait(v, i)
                rstd0.by(V.reciprocal(RSTD[:, gs], RT2[:, :, 0]))
                rstd0.wait(v, i)
                negm0.by(V.scalar_tensor_tensor(NEGM[:, gs], MV[:, gs, 0], -1.0, RSTD[:, gs], ALU.mult, ALU.mult))

            def find(t, q):
                if q == 0:
                    v.wait_ge(in_a[t % ABUF], 16 * (t // ABUF + 1))
                    if t >= LSLOTS:
                        node.wait(v, t - LSLOTS)
                found.by(V.max_index(IDX[:, t % LSLOTS, q, :], ones8[:], A[:, t % ABUF, q, :]))

            for t in range(GRP):
                v_stat(t)
            for i in range(NGRP):
                roots0(i)
                for t in range(i * GRP, (i + 1) * GRP):
                    if t + GRP < T:
                        v_stat(t + GRP)
                    n = t * NQ * LEAD // T
                    if (t + 1) * NQ * LEAD // T > n:
                        find(n // NQ, n % NQ)
                    turned0.wait(v, t)
                    if t >= 4:
                        g_ps.wait(v, t - 4)
                    ht0.by(V.tensor_copy(RT[:, t % 4, 0:KC, :].rearrange("p c n -> p (c n)"), bG[t % 2][:, 0:D]))
            g_sb.wait(v, T - 1)
            V.reduce_max(zs[:, 0:1], G[:, :, D], AX.X).then_inc(z_dve, 2)
            v.wait_ge(z_pool, 1)
            V.tensor_scalar_mul(zs[:, 2:3], zs[:, 1:2], -1.0).then_inc(z_dve, 1)
            v.wait_ge(z_pool, 2)
            V.reciprocal(zs[:, 5:6], zs[:, 4:5]).then_inc(z_dve, 1)
            v.wait_ge(z_dve, 4)
            V.tensor_scalar_mul(NATT[:], NATT[:], zs[:, 5:6]).then_inc(z_dve, 1)
            v.wait_ge(z_dve, 5)

            def number(t):
                s, z = t % LSLOTS, t % SLOTS
                found.wait(v, t)
                valid.by(V.tensor_scalar(VAL[:, s, :], IDX[:, s].rearrange("p q k -> p (q k)"), float(QC), None, ALU.is_lt))
                node.by(V.tensor_tensor(LST[:, z, L:2 * L].rearrange("p (q k) -> p q k", q=NQ), nbase[:], IDX[:, s], ALU.subtract))
                valid.wait(v, t)
                count.by(V.tensor_tensor_scan(CUM[:, t, :], VAL[:, s, :], VAL[:, s, :], 0.0, ALU.add, ALU.bypass))

            def positions(t):
                h = HALF[:, t:t + 1]
                count.wait(v, t)
                half.by(V.tensor_scalar(h, CUM[:, t, L - 1:L], 0.5, -0.5, ALU.mult, ALU.add))
                prefix.wait(v, t)
                place.by(V.scalar_tensor_tensor(LST[:, t % SLOTS, 0:L], CUM[:, t, :], PFX, VAL[:, t % LSLOTS, :], ALU.add, ALU.mult))
                half.wait(v, t)
                negc.by(V.tensor_scalar(NEGC[:, t:t + 1], PFX, h, -1.0, ALU.add, ALU.mult))

            def rows_matrix(t):
                dist.wait(v, t)
                rmat.by(V.tensor_scalar(R[:, t % SLOTS, :], DIST[:], HALF[:, t:t + 1], None, ALU.is_le))

            def lists(t):
                s = t % SLOTS
                pl = bI[:, 0:CH * (2 * L + 1)].rearrange("p (c k) -> p c k", c=CH)
                listed.wait(v, t)
                match.by(V.tensor_tensor(MAT[:, s], pl[:, :, 0:L], eown[:], ALU.is_equal))
                row.by(V.tensor_copy(ROW[:, t, :], pl[:, :, 2 * L]))
                match.wait(v, t)
                jm.by(V.tensor_tensor(tl[:], pl[:, :, L:2 * L], MAT[:, s], ALU.mult))
                jm.wait(v, t)
                jr.by(V.reduce_sum(js[:], tl[:], AX.X))
                jr.wait(v, t)
                nbr.by(V.tensor_scalar(NBR[:, t, :], js[:], -1.0, float(NONE), ALU.mult, ALU.add))

            def edge_matrix(t, signal):
                signal.by(V.tensor_tensor(RT[:, t % SLOTS], col1[:].unsqueeze(1).broadcast_to([P, CH, P]),
                                          ROW[:, t, :].unsqueeze(2).broadcast_to([P, CH, P]), ALU.is_equal))

            def scores(t, c):
                s = t % SLOTS
                n = 3 * t + c // 2
                gexp.wait(v, t, c // 2 + 1)
                v.wait_ge(gath[s], 16 * CH * (t // SLOTS + 1))
                if CH * t + c >= 2:
                    v.wait_ge(score.sem, CH * t + c - 1)
                score.by(V.tensor_tensor_reduce(out=prod[:, (CH * t + c) % 2], in0=bG[n % 3][:, (c % 2) * D:(c % 2 + 1) * D],
                                                in1=HJ[:, s, c, :], scale=1.0, scalar=0.0, op0=ALU.mult, op1=ALU.add,
                                                accum_out=sc[:, s, c:c + 1]))

            def place_scores(t):
                s = t % SLOTS
                V.tensor_scalar(PEN[:, s, :], VAL[:, t % LSLOTS, :], NEG_BIG, -NEG_BIG, ALU.mult, ALU.add)
                score.wait(v, t)
                scm.by(V.tensor_tensor(SM[:, s], MAT[:, s], sc[:, s, :].unsqueeze(2).broadcast_to([P, CH, L]), ALU.mult))

            def row_max(t):
                s = t % SLOTS
                srow.wait(v, t)
                smask.by(V.tensor_tensor(SR[:], PEN[:, s, :], SCR, ALU.subtract))
                smask.wait(v, t)
                smax.by(V.tensor_reduce(MS[:, s, 0:1], SR[:], AX.X, ALU.min))

            def row_scale(t):
                expd.wait(v, t)
                inv.by(V.reciprocal(rs[:], es[:]))
                inv.wait(v, t)
                rscale.by(V.tensor_tensor(MS[:, t % SLOTS, 1:2], rs[:], NATT[:, t:t + 1], ALU.mult))

            def edge_difference(t):
                msed.wait(v, t)
                diff.by(V.tensor_tensor(DF[:], sc[:, t % SLOTS, :], MSE[:, 0:2 * CH:2], ALU.add))

            def edge_weight(t):
                eexp.wait(v, t)
                wedge.by(V.tensor_tensor(WE[:, t % SLOTS, :], EE[:], MSE[:, 1:2 * CH:2], ALU.mult))

            def stats1(t):
                x1.wait(v, t)
                stat1.by(V.bn_stats(st[:, t % 2, :], X[:, t, :]))
                stat1.wait(v, t)
                aggr1.by(V.bn_aggr(MV[:, t, :], st[:, t % 2, :]))

            def norm_a(i):
                a, b = GROUPS[i]
                aggr1.wait(v, b - 1)
                V.tensor_scalar_add(VE[:, 0:b - a, 0], MV[:, a:b, 1], EPS)
                ve1.by(V.tensor_scalar_add(VE[:, 0:b - a, 1], DEG[:, a:b], 1.0))

            def norm_b(i):
                a, b = GROUPS[i]
                sq1.wait(v, i)
                inv1.by(V.reciprocal(RT2[:, 0:b - a], RT2[:, 0:b - a]))
                inv1.wait(v, i)
                V.tensor_copy(DINV[:, a:b], RT2[:, 0:b - a, 1])
                rd1.by(V.tensor_tensor(RSTD[:, a:b], RT2[:, 0:b - a, 0], RT2[:, 0:b - a, 1], ALU.mult))
                rd1.wait(v, i)
                nm1.by(V.scalar_tensor_tensor(NEGM[:, a:b], MV[:, a:b, 0], -1.0, RSTD[:, a:b], ALU.mult, ALU.mult))

            number(0)
            for i in range(T + 5):
                f, u, w, c, z = i + LEAD < T, i < T, 0 <= i - 2 < T, 0 <= i - 3 < T, 0 <= i - 5 < T
                if f:
                    find(i + LEAD, 0)
                if u:
                    positions(i)
                if c:
                    row_max(i - 3)
                if w:
                    scores(i - 2, 0)
                    scores(i - 2, 1)
                if z:
                    stats1(i - 5)
                for n, (_, b) in enumerate(GROUPS):
                    if b == i - 4:
                        norm_a(n)
                    if b == i - 5:
                        norm_b(n)
                if f:
                    find(i + LEAD, 1)
                if u:
                    rows_matrix(i)
                if c:
                    row_scale(i - 3)
                if w:
                    scores(i - 2, 2)
                    scores(i - 2, 3)
                if i + 1 < T:
                    number(i + 1)
                if w:
                    scores(i - 2, 4)
                if f:
                    find(i + LEAD, 2)
                if w:
                    edge_matrix(i - 2, rtm)
                    place_scores(i - 2)
                if c:
                    edge_difference(i - 3)
                if f:
                    find(i + LEAD, 3)
                if c:
                    edge_weight(i - 3)
                if u:
                    lists(i)
                if i - 4 == T:
                    norm_b(len(GROUPS) - 1)

            checked.wait(v, T - 1)
            V.tensor_reduce(badn[:], SQ[:], AX.X, ALU.add).then_inc(end_d, 1)
            v.wait_ge(end_d, 1)
            V.tensor_tensor(badm[:], badn[:], DEG[:], ALU.not_equal).then_inc(end_d, 1)
            v.wait_ge(end_d, 2)
            V.tensor_tensor(badn[:], HALF[:], NEGC[:], ALU.subtract).then_inc(end_d, 1)
            v.wait_ge(end_d, 3)
            V.scalar_tensor_tensor(badn[:], badn[:], float(EDGES - 1), badm[:], ALU.is_gt, ALU.max).then_inc(end_d, 1)
            v.wait_ge(end_d, 4)
            V.reduce_max(zs[:, 6:7], badn[:], AX.X).then_inc(end_d, 1)

            for t in range(T + 2):
                if t < T:
                    if t >= SLOTS:
                        y_ps.wait(v, t - SLOTS)
                    else:
                        zt_ps.wait(v, T - SLOTS + t)
                    edge_matrix(t, rt1)
                if t >= 2:
                    n = t - 2
                    o1_sb.wait(v, n)
                    if n >= 2:
                        v.wait_ge(stored[n % 2], 16 * (n // 2))
                    o_add.by(V.tensor_tensor(OT[:, n % 2, :], Y2[:, n % 2, :], X[:, n, :], ALU.add))
            v.wait_ge(end_p, 1)
            V.tensor_copy(flag[:], zs[:, 7:8]).then_inc(end_d, 1)
            v.wait_ge(end_d, 6)

        @block.scalar
        def _(a):
            S_ = nc.scalar

            def squares(t, j):
                if j == 0:
                    a.wait_ge(in_a[t % ABUF], 16 * (t // ABUF + 1))
                if 2 * t + j >= 1:
                    a.wait_ge(checked.sem, 2 * t + j)
                n = NQ // 2
                checked.by(S_.activation(junk[:], A[:, t % ABUF, j * n:(j + 1) * n, 0:QC], ACT.Square, accum_out=SQ[:, t, j:j + 1]))

            for i in range(NGRP):
                ve0.wait(a, i)
                sq0.by(S_.activation(RT2[:, :, 0], VE[:, :, 0], ACT.Sqrt))
                negm0.wait(a, i)
                if i >= 2:
                    a.wait_ge(stored0[i % 2], 16 * (i // 2))
                for t in range(i * GRP, (i + 1) * GRP):
                    h0.by(S_.activation(HST[:, i % 2, t % GRP, :], X[:, t, :], ACT.Relu, bias=NEGM[:, t:t + 1], scale=RSTD[:, t:t + 1]))
                    if t >= 4:
                        g_keep(a, t - 4)
                    n = t * 2 * LEAD // T
                    if (t + 1) * 2 * LEAD // T > n:
                        squares(n // 2, n % 2)
            for t in range(T - 4, T):
                g_keep(a, t)
            a.wait_ge(z_dve, 3)
            S_.activation(NATT[:], G[:, :, D], ACT.Exp, bias=zs[:, 2:3], accum_out=zs[:, 3:4]).then_inc(z_act, 1)

            def distance(t):
                negc.wait(a, t)
                if t >= 1:
                    rmat.wait(a, t - 1)
                dist.by(S_.activation(DIST[:], epos[:], ACT.Abs, bias=NEGC[:, t:t + 1]))

            def exponent(t):
                smax.wait(a, t)
                if t >= 1:
                    inv.wait(a, t - 1)
                expd.by(S_.activation(EX[:], SR[:], ACT.Exp, bias=MS[:, t % SLOTS, 0:1], scale=-1.0, accum_out=es[:]))

            def edge_exponent(t):
                diff.wait(a, t)
                eexp.by(S_.activation(EE[:], DF[:], ACT.Exp))

            def weigh(t):
                wedge.wait(a, t)
                if t >= 2:
                    zt_ps.wait(a, t - 2)
                for c in range(CH):
                    ins = S_.activation(RW[:, t % 2, c, :], RT[:, t % SLOTS, c, :], ACT.Copy, scale=WE[:, t % SLOTS, c:c + 1])
                rw.by(ins)

            def keep_z(t):
                zt_ps.wait(a, t)
                if t >= 2:
                    o_ps.wait(a, t - 2)
                zt_sb.by(S_.copy(ZT[:, t % 2].rearrange("p c n -> p (c n)"), bZ[:, 0:D]))

            def keep_x1(t):
                o_ps.wait(a, t)
                x1.by(S_.copy(X[:, t, :], bO[:, 0:D]))

            def next_h(t):
                for n, (b, _) in enumerate(GROUPS):
                    if b == t:
                        nm1.wait(a, n)
                h1.by(S_.activation(G[:, t, 0:D], X[:, t, :], ACT.Relu, bias=NEGM[:, t:t + 1], scale=RSTD[:, t:t + 1]))

            made = 0
            ready = 0
            for i in range(T + 5):
                y, last = 0 <= i - 4 < T, i - 3 == T - 1
                if y and i - 4 < T - 1:
                    weigh(i - 4)
                if i < T:
                    distance(i)
                if 0 <= i - 3 < T:
                    exponent(i - 3)
                if i + LEAD < T:
                    squares(i + LEAD, 0)
                if last:
                    edge_exponent(T - 1)
                    weigh(T - 1)
                if i - 4 == T - 1:
                    for t in (made, made + 1):
                        next_h(t)
                    keep_z(T - 1)
                    for t in (made + 2, made + 3):
                        next_h(t)
                    made += 4
                elif y:
                    keep_z(i - 4)
                if i + LEAD < T:
                    squares(i + LEAD, 1)
                if 0 <= i - 3 < T and not last:
                    edge_exponent(i - 3)
                if y:
                    keep_x1(i - 4)
                for _ in range(2 if i + LEAD >= T else 1):
                    if made < ready and i - 4 < T - 1:
                        next_h(made)
                        made += 1
                for n, (b, e) in enumerate(GROUPS):
                    if e == i - 4:
                        while made < ready and e < T:
                            next_h(made)
                            made += 1
                        ve1.wait(a, n)
                        sq1.by(S_.activation(RT2[:, 0:e - b], VE[:, 0:e - b], ACT.Sqrt))
                        ready = e
            while made < T:
                next_h(made)
                made += 1
            for t in range(T + 1):
                if t < T:
                    y_ps.wait(a, t)
                    if t >= 2:
                        o1_ps.wait(a, t - 2)
                    y_sb.by(S_.copy(ZT[:, t % 2].rearrange("p c n -> p (c n)"), (bZ, bG[0])[t % 2][:, 0:D]))
                if t >= 1:
                    n = t - 1
                    o1_ps.wait(a, n)
                    if n >= 2:
                        o_add.wait(a, n - 2)
                    o1_sb.by(S_.activation(Y2[:, n % 2, :], (bO, bI)[n % 2][:, 0:D], ACT.Relu, scale=DINV[:, n:n + 1]))

        @block.tensor
        def _(pe):
            MM = nc.tensor.matmul
            pe.wait_ge(c_dve, 4)
            pe.wait_ge(in_e, 16)
            for k in range(KC):
                for d in range(KC):
                    mm = nc.tensor.transpose(bZ[:, d * D + k * P:d * D + (k + 1) * P], EW[:, k, d * P:(d + 1) * P], ident[:])
            mm.then_inc(ewt_ps, 1)
            pe.wait_ge(ewt_sb, 1)
            for k in range(KC):
                for d in range(KC):
                    mm = MM(bI[:, k * D:(k + 1) * D], EWT[:, d, k * P:(k + 1) * P], EWT[:, d, :], start=d == 0, stop=d == KC - 1)
            mm.then_inc(m_ps, 1)
            pe.wait_ge(m_sb, 1)
            pe.wait_ge(in_w, 64)

            def turn0(t):
                h0.wait(pe, t)
                if t >= 2:
                    ht0.wait(pe, t - 2)
                for c in range(KC):
                    mm = nc.tensor.transpose(bG[t % 2][:, c * P:(c + 1) * P], HST[:, t // GRP % 2, t % GRP, c * P:(c + 1) * P], ident[:])
                turned0.by(mm)

            def product0(t):
                ht0.wait(pe, t)
                if t >= 4:
                    g_sb.wait(pe, t - 4)
                for c in range(KC):
                    mm = MM((bO, bZ, bR, bG[2])[t % 4][:, 0:GW], RT[:, t % 4, c, :], MZ[:, c, :], start=c == 0, stop=c == KC - 1)
                g_ps.by(mm)

            for t in range(T + 1):
                if t < T:
                    turn0(t)
                if t >= 1:
                    product0(t - 1)
            g_sb.wait(pe, T - 1)
            pe.wait_ge(c_dve, 5)

            def g_edges(t, j):
                n = 3 * t + j
                if n >= 3:
                    v = n - 3
                    pe.wait_ge(score.sem, 5 * (v // 3) + min(2 * (v % 3) + 2, CH))
                for c in range(2 * j, min(2 * j + 2, CH)):
                    mm = MM(bG[n % 3][:, (c % 2) * D:(c % 2 + 1) * D], R[:, t % SLOTS, c * P:(c + 1) * P], G[:, t, 0:D], start=True, stop=True)
                gexp.by(mm)

            def prefixes(t):
                count.wait(pe, t)
                if t >= 1:
                    negc.wait(pe, t - 1)
                prefix.by(MM(PFX, below[:], CUM[:, t, L - 1:L], start=True, stop=True))

            def weighted(t):
                rw.wait(pe, t)
                if t >= 1:
                    zt_sb.wait(pe, t - 1)
                for d in range(KC):
                    for c in range(CH):
                        mm = MM(bZ[:, d * P:(d + 1) * P], HJ[:, t % SLOTS, c, d * P:(d + 1) * P], RW[:, t % 2, c, :], start=c == 0, stop=c == CH - 1)
                zt_ps.by(mm)

            def attended(t):
                if t >= 1:
                    x1.wait(pe, t - 1)
                MM(bO[:, 0:D], ident[:], X[:, t, :], start=True, stop=False)
                MM(bO[:, 0:D], ones_row[:], BIAS[:], start=False, stop=False)
                zt_sb.wait(pe, t)
                for d in range(KC):
                    mm = MM(bO[:, 0:D], ZT[:, t % 2, d, :], W0[:, d, :], start=False, stop=d == KC - 1)
                o_ps.by(mm)

            def by_row(t):
                scm.wait(pe, t)
                rtm.wait(pe, t)
                if t >= 1:
                    wedge.wait(pe, t - 1)
                for c in range(CH):
                    mm = MM(SCR, RT[:, t % SLOTS, c, :], SM[:, t % SLOTS, c, :], start=c == 0, stop=c == CH - 1)
                srow.by(mm)

            def to_edges(t):
                rmat.wait(pe, t)
                if t >= 1:
                    jm.wait(pe, t - 1)
                place.wait(pe, t)
                K = 2 * L + 1
                for c in range(CH):
                    mm = MM(bI[:, c * K:(c + 1) * K], R[:, t % SLOTS, c * P:(c + 1) * P], LST[:, t % SLOTS, :], start=True, stop=True)
                listed.by(mm)

            def scale_edges(t):
                rscale.wait(pe, t)
                for c in range(CH):
                    mm = MM(MSE[:, 2 * c:2 * c + 2], R[:, t % SLOTS, c * P:(c + 1) * P], MS[:, t % SLOTS, :], start=True, stop=True)
                msed.by(mm)

            pe.wait_ge(c_dve, 5 + SLOTS)
            prefixes(0)
            for i in range(T + 4):
                if 0 <= i - 2 < T:
                    for j in range(3):
                        g_edges(i - 2, j)
                if 0 <= i - 4 < T:
                    weighted(i - 4)
                if 0 <= i - 3 < T:
                    scale_edges(i - 3)
                if i < T:
                    to_edges(i)
                if i + 1 < T:
                    prefixes(i + 1)
                if 0 <= i - 4 < T:
                    attended(i - 4)
                if 0 <= i - 2 < T:
                    by_row(i - 2)

            def gathered_sum(t):
                s = t % SLOTS
                pe.wait_ge(g1[s], 16 * CH * (t // SLOTS + 1))
                rt1.wait(pe, t)
                if t >= 2:
                    y_sb.wait(pe, t - 2)
                b = (bZ, bG[0])[t % 2]
                for d in range(KC):
                    MM(b[:, d * P:(d + 1) * P], G[:, t, d * P:(d + 1) * P], ident[:], start=True, stop=False)
                    for c in range(CH):
                        mm = MM(b[:, d * P:(d + 1) * P], HJ[:, s, c, d * P:(d + 1) * P], RT[:, s, c, :], start=False, stop=c == CH - 1)
                y_ps.by(mm)

            def convolved(t):
                y_sb.wait(pe, t)
                if t >= 2:
                    o1_sb.wait(pe, t - 2)
                for d in range(KC):
                    mm = MM((bO, bI)[t % 2][:, 0:D], ZT[:, t % 2, d, :], W1[:, d, :], start=d == 0, stop=d == KC - 1)
                o1_ps.by(mm)

            h1.wait(pe, T - 1)
            for t in range(T + 1):
                if t < T:
                    gathered_sum(t)
                if t >= 1:
                    convolved(t - 1)


class Chain:

    def __init__(self, sem, per=0, base=0):
        self.sem, self.per, self.base, self.n = sem, per, base, 0

    def done(self, ins):
        self.n += 1
        ins.then_inc(self.sem, 1)

    def at(self, turn, k):
        return turn * self.per + (self.base + k)

    def link(self, eng, turn, ins):
        self.done(ins)
        eng.wait_ge(self.sem, self.at(turn, self.n))


def general_path(nc, flag, x, adj, w0, bias, node_w, edge_w, w1, out, table):
    adj_t = adj.rearrange("(t p) n -> t p n", p=P)
    table_t = table.rearrange("(t p) d -> t p d", p=P)
    out_t = out.rearrange("(t p) d -> t p d", p=P)
    with ExitStack() as ctx:
        def sb(name, shape, dt=F32):
            return ctx.enter_context(nc.sbuf_tensor("general_" + name, shape, dt))

        def ps(name):
            return ctx.enter_context(nc.psum_tensor("general_" + name, [P, SC], F32))

        def sem(name):
            return ctx.enter_context(nc.semaphore(name))

        X = sb("X", [P, T, D])
        QT = sb("QT", [P, KC, N])
        SUP = sb("SUP", [P, T, D])
        AT = sb("AT", [P, N])
        S = sb("S", [P, N])
        PT = sb("PT", [P, 2, SC])
        W0 = sb("W0", [P, KC, D])
        EW = sb("EW", [P, KC, D])
        W1 = sb("W1", [P, KC, D])
        NW = sb("NW", [P, KC])
        BIAS = sb("BIAS", [P, D])
        ident = sb("ident", [P, P])
        xc = sb("xc", [P, D])
        hn = sb("hn", [P, D])
        hT = sb("hT", [P, KC, P])
        qs = sb("qs", [P, KC, P])
        tmp = sb("tmp", [P, SC])
        Z = sb("Z", [P, T])
        NATT = sb("NATT", [P, T])
        DI = sb("DI", [P, T])
        sm = sb("sm", [P, 16])
        c1 = lambda i: sm[:, i:i + 1]
        psS = [ps(f"psS{i}") for i in range(2)]
        psT = [ps(f"psT{i}") for i in range(2)]
        psQ, psO, psZ = ps("psQ"), ps("psO"), ps("psZ")

        g_in = sem("g_inputs")
        g_adj = sem("g_adj")
        g_id = sem("g_identity")
        g_tab = sem("g_table")
        g_back = sem("g_table_back")
        g_out = sem("g_out")
        g_pool = sem("g_pool")
        dsem = [sem(f"g_dve{i}") for i in range(4)]
        asem = [sem(f"g_act{i}") for i in range(4)]
        psem = [sem(f"g_pe{i}") for i in range(4)]
        D1, D2, D3 = 10, 45, 3
        A1, A2, A3 = 3, 11, 9
        P1, P2, P3 = 2, 17, 18
        block = ctx.enter_context(nc.Block())

        def layernorm(v, ch, t, src, act_sem, act_at):
            ch.link(v, t, nc.vector.tensor_scalar_mul(xc[:], src, 1.0))
            ch.link(v, t, nc.vector.reduce_sum(c1(0), xc[:], AX.X))
            ch.link(v, t, nc.vector.tensor_scalar_mul(c1(1), c1(0), -1.0 / D))
            ch.link(v, t, nc.vector.tensor_scalar_add(xc[:], xc[:], c1(1)))
            ch.link(v, t, nc.vector.tensor_tensor_reduce(out=tmp[:, 0:D], in0=xc[:], in1=xc[:], scale=1.0, scalar=0.0,
                                                         op0=ALU.mult, op1=ALU.add, accum_out=c1(2)))
            ch.link(v, t, nc.vector.tensor_scalar(c1(3), c1(2), 1.0 / D, EPS, ALU.mult, ALU.add))
            v.wait_ge(act_sem, act_at)
            ch.link(v, t, nc.vector.reciprocal(c1(5), c1(4)))
            ch.link(v, t, nc.vector.tensor_scalar(hn[:], xc[:], c1(5), 0.0, ALU.mult, ALU.max))

        @block.sync
        def _(sp):
            wanted = sp.value_load(flag[0:1, 0:1])
            with sp.If(wanted > 0):
                sp.sem_inc(dsem[2], D2)
                sp.sem_inc(psem[3], P3)
                sp.sem_inc(asem[3], A3)
                sp.sem_inc(g_tab, 16)
                sp.sem_inc(g_out, 16)
                sp.dma_start(X[:], x.rearrange("(t p) d -> p t d", p=P)).then_inc(g_in, 16)
                for dst, src in ((W0, w0), (EW, edge_w), (W1, w1)):
                    sp.dma_start(dst[:], src.rearrange("(c p) n -> p c n", p=P)).then_inc(g_in, 16)
                with nc.allow_non_contiguous_dma(reason="256 values of the node weights"):
                    sp.dma_start(NW[:], node_w.rearrange("(c p) o -> p (c o)", p=P)).then_inc(g_in, 16)
                sp.dma_start(BIAS[:], bias.rearrange("(o n) -> o n", o=1).broadcast_to([P, D])).then_inc(g_in, 16)
                with sp.Fori(0, T) as t:
                    sp.wait_ge(dsem[2], t * D2 + D2)
                    sp.dma_start(AT[:], adj_t[t]).then_inc(g_adj, 16)
                    sp.wait_ge(dsem[2], t * D2 + D2 + D2)
                    sp.dma_start(table_t[t], hn[:]).then_inc(g_tab, 16)
                sp.wait_ge(g_tab, 16 * (T + 1))
                sp.wait_ge(psem[2], T * P2)
                sp.dma_start(SUP[:], table.rearrange("(t p) d -> p t d", p=P)).then_inc(g_back, 16)
                with sp.Fori(0, T) as t:
                    sp.wait_ge(psem[3], t * P3 + P3)
                    sp.dma_start(AT[:], adj_t[t]).then_inc(g_adj, 16)
                    sp.wait_ge(dsem[3], t * D3 + D3)
                    sp.dma_start(out_t[t], hn[:]).then_inc(g_out, 16)
                sp.wait_ge(g_out, 16 * (T + 1))
            sp.nop()

        @block.gpsimd
        def _(g):
            wanted = g.value_load(flag[0:1, 0:1])
            with g.If(wanted > 0):
                g.memset(ident[:], 0.0).then_inc(g_id, 1)
                g.wait_ge(g_id, 1)
                g.affine_select(out=ident[:], in_=ident[:], compare_op=ALU.not_equal, fill=1.0, base=0,
                                pattern=[[-1, P]], channel_multiplier=1).then_inc(g_id, 1)
                g.wait_ge(dsem[1], 1)
                g.partition_all_reduce(c1(7), c1(6), P, bass.bass_isa.ReduceOp.max).then_inc(g_pool, 1)
                g.wait_ge(asem[1], 1)
                g.partition_all_reduce(c1(10), c1(9), P, bass.bass_isa.ReduceOp.add).then_inc(g_pool, 1)
            g.nop()

        @block.vector
        def _(v):
            wanted = v.value_load(flag[0:1, 0:1])
            with v.If(wanted > 0):
                v.wait_ge(g_in, 96)
                ch = Chain(dsem[0], D1)
                with v.Fori(0, T) as t:
                    ch.n = 0
                    layernorm(v, ch, t, X[:, t, :], asem[0], t * A1 + 1)
                    v.wait_ge(psem[0], t * P1 + 2)
                    ch.done(nc.vector.tensor_copy(SUP[:, t, :], psO[:, 0:D]))
                    ch.link(v, t, nc.vector.tensor_copy(Z[:, bass.ds(t, 1)], psZ[:, 0:1]))
                    assert ch.n == D1
                ch = Chain(dsem[1])
                ch.link(v, 0, nc.vector.reduce_max(c1(6), Z[:], AX.X))
                v.wait_ge(g_pool, 1)
                ch.link(v, 0, nc.vector.tensor_scalar_mul(c1(8), c1(7), -1.0))
                v.wait_ge(g_pool, 2)
                ch.link(v, 0, nc.vector.reciprocal(c1(11), c1(10)))
                v.wait_ge(asem[1], 1)
                ch.link(v, 0, nc.vector.tensor_scalar_mul(NATT[:], NATT[:], c1(11)))

                ch = Chain(dsem[2], D2, D2)
                with v.Fori(0, T) as t:
                    ch.n = 0
                    v.wait_ge(g_adj, t * 16 + 16)
                    ch.done(nc.vector.tensor_copy(qs[:], QT[:, :, bass.ds(t * P, P)]))
                    ch.link(v, t, nc.vector.reduce_sum(c1(12), AT[:], AX.X))
                    for c in range(NS):
                        cs = slice(c * SC, (c + 1) * SC)
                        ch.link(v, t, nc.vector.tensor_scalar(tmp[:], AT[:, cs], 0.0, -NEG_BIG, ALU.is_gt, ALU.mult))
                        v.wait_ge(psem[2], t * P2 + c + 1)
                        ch.link(v, t, nc.vector.scalar_tensor_tensor(S[:, cs], AT[:, cs], 0.0, psS[c % 2][:], ALU.is_gt, ALU.mult))
                        ch.link(v, t, nc.vector.scalar_tensor_tensor(S[:, cs], tmp[:], NEG_BIG, S[:, cs], ALU.add, ALU.add))
                    ch.link(v, t, nc.vector.reduce_max(c1(6), S[:], AX.X))
                    ch.link(v, t, nc.vector.tensor_scalar_mul(c1(8), c1(6), -1.0))
                    v.wait_ge(asem[2], t * A2 + 1)
                    ch.link(v, t, nc.vector.tensor_tensor(S[:], S[:], AT[:], ALU.mult))
                    ch.link(v, t, nc.vector.reciprocal(c1(10), c1(9)))
                    ch.link(v, t, nc.vector.tensor_tensor(c1(11), c1(10), NATT[:, bass.ds(t, 1)], ALU.mult))
                    v.wait_ge(psem[2], t * P2 + P2)
                    ch.link(v, t, nc.vector.scalar_tensor_tensor(tmp[:, 0:D], psO[:, 0:D], c1(11), BIAS[:], ALU.mult, ALU.add))
                    ch.link(v, t, nc.vector.tensor_tensor(X[:, t, :], X[:, t, :], tmp[:, 0:D], ALU.add))
                    v.wait_ge(g_tab, t * 16 + 16)
                    layernorm(v, ch, t, X[:, t, :], asem[2], t * A2 + 10)
                    ch.link(v, t, nc.vector.tensor_scalar_add(c1(13), c1(12), 1.0))
                    v.wait_ge(asem[2], t * A2 + 11)
                    ch.link(v, t, nc.vector.reciprocal(c1(15), c1(14)))
                    ch.done(nc.vector.tensor_copy(DI[:, bass.ds(t, 1)], c1(15)))
                    ch.link(v, t, nc.vector.tensor_scalar_mul(hn[:], hn[:], c1(15)))
                    assert ch.n == D2, ch.n

                ch = Chain(dsem[3], D3)
                v.wait_ge(g_back, 16)
                v.wait_ge(g_tab, 16 * (T + 1))
                with v.Fori(0, T) as t:
                    ch.n = 0
                    v.wait_ge(psem[3], t * P3 + P3 + 16)
                    ch.link(v, t, nc.vector.tensor_tensor(xc[:], psO[:, 0:D], SUP[:, t, :], ALU.add))
                    ch.link(v, t, nc.vector.tensor_scalar_mul(xc[:], xc[:], DI[:, bass.ds(t, 1)]))
                    v.wait_ge(psem[3], t * P3 + P3 + P3)
                    v.wait_ge(g_out, t * 16 + 16)
                    ch.link(v, t, nc.vector.scalar_tensor_tensor(hn[:], psQ[:, 0:D], 0.0, X[:, t, :], ALU.max, ALU.add))
                    assert ch.n == D3, ch.n
            v.nop()

        @block.scalar
        def _(a):
            wanted = a.value_load(flag[0:1, 0:1])
            with a.If(wanted > 0):
                with a.Fori(0, T) as t:
                    a.wait_ge(dsem[0], t * D1 + 6)
                    nc.scalar.activation(c1(4), c1(3), ACT.Sqrt).then_inc(asem[0], 1)
                    a.wait_ge(psem[0], t * P1 + 1)
                    nc.scalar.copy(hT[:].rearrange("p c n -> p (c n)"), psT[0][:, 0:D]).then_inc(asem[0], 1)
                    a.wait_ge(psem[0], t * P1 + 2)
                    nc.scalar.copy(QT[:, :, bass.ds(t * P, P)], psQ[:, 0:D].rearrange("p (c n) -> p c n", c=KC)).then_inc(asem[0], 1)
                a.wait_ge(dsem[1], 2)
                nc.scalar.activation(NATT[:], Z[:], ACT.Exp, bias=c1(8), accum_out=c1(9)).then_inc(asem[1], 1)
                with a.Fori(0, T) as t:
                    a.wait_ge(dsem[2], t * D2 + D2 + 28)
                    nc.scalar.activation(S[:], S[:], ACT.Exp, bias=c1(8), accum_out=c1(9)).then_inc(asem[2], 1)
                    for g in range(NS):
                        a.wait_ge(psem[2], t * P2 + 8 + g + 1)
                        nc.scalar.copy(PT[:, g % 2, :], psT[g % 2][:]).then_inc(asem[2], 1)
                    a.wait_ge(dsem[2], t * D2 + D2 + 39)
                    nc.scalar.activation(c1(4), c1(3), ACT.Sqrt).then_inc(asem[2], 1)
                    a.wait_ge(dsem[2], t * D2 + D2 + 42)
                    nc.scalar.activation(c1(14), c1(13), ACT.Sqrt).then_inc(asem[2], 1)
                with a.Fori(0, T) as t:
                    for g in range(NS):
                        a.wait_ge(psem[3], t * P3 + P3 + g + 1 + (g > 0) * (g - 1))
                        nc.scalar.copy(PT[:, g % 2, :], psT[g % 2][:]).then_inc(asem[3], 1)
                    a.wait_ge(psem[3], t * P3 + P3 + 17)
                    nc.scalar.copy(hT[:].rearrange("p c n -> p (c n)"), psT[0][:, 0:D]).then_inc(asem[3], 1)
            a.nop()

        @block.tensor
        def _(pe):
            wanted = pe.value_load(flag[0:1, 0:1])
            with pe.If(wanted > 0):
                pe.wait_ge(g_id, 2)
                pe.wait_ge(g_in, 96)

                def turn(src):
                    for c in range(KC):
                        mm = nc.tensor.transpose(psT[0][:, c * P:(c + 1) * P], src[:, c * P:(c + 1) * P], ident[:])
                    return mm

                with pe.Fori(0, T) as t:
                    pe.wait_ge(dsem[0], t * D1 + 8)
                    turn(hn).then_inc(psem[0], 1)
                    pe.wait_ge(asem[0], t * A1 + 2)
                    for d in range(KC):
                        for c in range(KC):
                            nc.tensor.matmul(psQ[:, d * P:(d + 1) * P], EW[:, c, d * P:(d + 1) * P], hT[:, c, :], start=c == 0, stop=c == KC - 1)
                    for c in range(KC):
                        nc.tensor.matmul(psO[:, 0:D], hT[:, c, :], W0[:, c, :], start=c == 0, stop=c == KC - 1)
                    for c in range(KC):
                        mm = nc.tensor.matmul(psZ[:, 0:1], hT[:, c, :], NW[:, c:c + 1], start=c == 0, stop=c == KC - 1)
                    mm.then_inc(psem[0], 1)
                    pe.wait_ge(asem[0], t * A1 + 3)

                def transposes(src, g):
                    for k in range(SC // P):
                        b = g * (SC // P) + k
                        mm = nc.tensor.transpose(psT[g % 2][:, k * P:(k + 1) * P], src[:, b * P:(b + 1) * P], ident[:])
                    return mm

                def products(g):
                    for k in range(SC // P):
                        b = g * (SC // P) + k
                        mm = nc.tensor.matmul(psO[:, 0:D], PT[:, g % 2, k * P:(k + 1) * P], SUP[:, b, :], start=b == 0, stop=b == T - 1)
                    return mm

                pe.wait_ge(dsem[0], T * D1)
                with pe.Fori(0, T) as t:
                    pe.wait_ge(dsem[2], t * D2 + D2 + 2)
                    for c in range(NS):
                        if c >= 2:
                            pe.wait_ge(dsem[2], t * D2 + D2 + 2 + 3 * (c - 2) + 2)
                        for k in range(KC):
                            mm = nc.tensor.matmul(psS[c % 2][:], qs[:, k, :], QT[:, k, c * SC:(c + 1) * SC], start=k == 0, stop=k == KC - 1)
                        mm.then_inc(psem[2], 1)
                    pe.wait_ge(dsem[2], t * D2 + D2 + 29)
                    transposes(S, 0).then_inc(psem[2], 1)
                    for g in range(NS):
                        if g + 1 < NS:
                            if g >= 1:
                                pe.wait_ge(asem[2], t * A2 + 1 + g)
                            transposes(S, g + 1).then_inc(psem[2], 1)
                        pe.wait_ge(asem[2], t * A2 + 1 + g + 1)
                        mm = products(g)
                    mm.then_inc(psem[2], 1)
                pe.wait_ge(g_back, 16)
                with pe.Fori(0, T) as t:
                    pe.wait_ge(g_adj, t * 16 + 16 * (T + 1))
                    pe.wait_ge(asem[3], t * A3 + A3)
                    transposes(AT, 0).then_inc(psem[3], 1)
                    for g in range(NS):
                        if g + 1 < NS:
                            if g >= 1:
                                pe.wait_ge(asem[3], t * A3 + A3 + g)
                            transposes(AT, g + 1).then_inc(psem[3], 1)
                        pe.wait_ge(asem[3], t * A3 + A3 + g + 1)
                        products(g).then_inc(psem[3], 1)
                    pe.wait_ge(dsem[3], t * D3 + 2)
                    turn(xc).then_inc(psem[3], 1)
                    pe.wait_ge(asem[3], t * A3 + A3 + 9)
                    for c in range(KC):
                        mm = nc.tensor.matmul(psQ[:, 0:D], hT[:, c, :], W1[:, c, :], start=c == 0, stop=c == KC - 1)
                    mm.then_inc(psem[3], 1)
                    pe.wait_ge(dsem[3], t * D3 + 3)
            pe.nop()


def build(nc, x, adj, w0, bias, node_w, edge_w, w1, out):
    with nc.sbuf_tensor("flag", [P, 1], I32) as flag:
        table0 = nc.dram_tensor("h0_rows", [N, D], F32, kind="Internal").ap()
        table1 = nc.dram_tensor("h1_rows", [N, D], F32, kind="Internal").ap()
        edge_path(nc, flag, x, adj, w0, bias, node_w, edge_w, w1, out, table0, table1)
        general_path(nc, flag, x, adj, w0, bias, node_w, edge_w, w1, out, table1)


_INS = ["x", "adj", "L0_gnn_weight", "L0_gnn_bias", "L0_gnn_node_w", "L0_gnn_edge_w", "L1_gnn_W"]


def kernel(**inputs):
    import numpy as _np
    import concourse.bacc as _bacc
    from concourse import mybir as _mybir
    from concourse.bass_utils import run_bass_kernel_spmd as _run

    nc = _bacc.Bacc("TRN2", target_bir_lowering=False, num_devices=1)
    arrays, args = {}, []
    for name in _INS:
        a = _np.ascontiguousarray(inputs[name])
        arrays[f"in_{name}_dram"] = a
        args.append(nc.dram_tensor(f"in_{name}_dram", a.shape, _mybir.dt.from_np(a.dtype), kind="ExternalInput").ap())
    args.append(nc.dram_tensor("out_0_dram", (N, D), _mybir.dt.float32, kind="ExternalOutput").ap())
    build(nc, *args)
    r = _run(nc, [arrays], core_ids=[0])
    return r.results[0]["out_0_dram"]
```
